# Optimizing a Trainium2 kernel written in Bass

```python
import numpy as np
import jax
import jax.numpy as jnp

def _softmax(x, axis=-1):
    return jax.nn.softmax(x, axis=axis)

def _gelu(x):
    return jax.nn.gelu(x, approximate=True)

def _silu(x):
    return jax.nn.silu(x)

def _sigmoid(x):
    return jax.nn.sigmoid(x)

def _layernorm(x, axis=-1, eps=1e-05):
    m = jnp.mean(x, axis=axis, keepdims=True)
    v = jnp.var(x, axis=axis, keepdims=True)
    return (x - m) / jnp.sqrt(v + eps)

def _scatter_add(tgt, idx, src, axis=0):
    return tgt.at[idx].add(src)

def _segment_sum(src, seg, n):
    return jax.ops.segment_sum(src, seg, n)
kernel_name = 'mk_adaln_d1_jaxref_r8_846b46'

def setup_inputs(seed: int=0):
    np.random.seed(seed)
    _w = jnp.asarray

    def _L0_attn_setup():
        import jax, jax.numpy as jnp
        import numpy as np
        N_FILTERS = 128
        N_HEADS = 16
        key = jax.random.key(seed)
        k1, k2, k3 = jax.random.split(key, 3)
        x = jax.random.normal(k1, (8, 128, N_FILTERS), dtype=jnp.float32)
        w_qkv = jax.random.normal(k2, (N_FILTERS, N_FILTERS * 3), dtype=jnp.float32) * (0.02 / N_FILTERS) ** 0.5
        w_out = jax.random.normal(k3, (N_FILTERS, N_FILTERS), dtype=jnp.float32) * (0.02 / N_FILTERS) ** 0.5
        return {'x': x, 'w_qkv': w_qkv, 'w_out': w_out}
    _L0_attn_in = _L0_attn_setup()

    def _L0_ffn_setup():
        import jax, jax.numpy as jnp
        import numpy as np
        TOP_K = 2
        EPS = 1e-20

        def _moe(x, w_router, w_gate, w_up, w_down):
            B, S, D = x.shape
            E = w_router.shape[1]
            xf = x.reshape(-1, D)
            T = xf.shape[0]
            scores = jax.nn.softmax(xf @ w_router, axis=-1)
            topk_w, topk_idx = jax.lax.top_k(scores, TOP_K)
            topk_w = topk_w / (jnp.sum(topk_w, axis=-1, keepdims=True) + EPS)
            comb = jnp.zeros((T, E), dtype=xf.dtype).at[jnp.arange(T)[:, None], topk_idx].set(topk_w)
            g = jnp.einsum('td,edh->eth', xf, w_gate)
            u = jnp.einsum('td,edh->eth', xf, w_up)
            h = jax.nn.silu(g) * u
            out_e = jnp.einsum('eth,ehd->etd', h, w_down)
            y = jnp.einsum('etd,te->td', out_e, comb)
            return y.reshape(B, S, D)
        key = jax.random.key(seed)
        ks = jax.random.split(key, 5)
        B, S, D, E, H = (2, 256, 128, 8, 176)
        sd = 1.0 / np.sqrt(D)
        sh = 1.0 / np.sqrt(H)
        return {'x': jax.random.normal(ks[0], (B, S, D), dtype=jnp.float32), 'w_router': jax.random.normal(ks[1], (D, E), dtype=jnp.float32) * sd, 'w_gate': jax.random.normal(ks[2], (E, D, H), dtype=jnp.float32) * sd, 'w_up': jax.random.normal(ks[3], (E, D, H), dtype=jnp.float32) * sd, 'w_down': jax.random.normal(ks[4], (E, H, D), dtype=jnp.float32) * sh}
    _L0_ffn_in = _L0_ffn_setup()
    _L0_c = _w((lambda *s: np.random.randn(*s).astype(np.float32) * 0.05)(8, 128))
    _L0_wmod = _w((lambda *s: np.random.randn(*s).astype(np.float32) * 0.05)(128, 6 * 128) * 128 ** (-0.5))
    _d = {'L0_attn_x': _L0_attn_in['x'], 'L0_attn_w_qkv': _L0_attn_in['w_qkv'], 'L0_attn_w_out': _L0_attn_in['w_out'], 'L0_ffn_w_router': _L0_ffn_in['w_router'], 'L0_ffn_w_gate': _L0_ffn_in['w_gate'], 'L0_ffn_w_up': _L0_ffn_in['w_up'], 'L0_ffn_w_down': _L0_ffn_in['w_down'], 'L0_c': _L0_c, 'L0_wmod': _L0_wmod}
    _x0 = _d['L0_attn_x']
    _d['L0_attn_x'] = jax.random.normal(jax.random.fold_in(jax.random.key(seed), 1), (8, 512, 128), dtype=_x0.dtype)
    del _x0
    return _d

def reference(L0_attn_x, L0_attn_w_qkv, L0_attn_w_out, L0_ffn_w_router, L0_ffn_w_gate, L0_ffn_w_up, L0_ffn_w_down, L0_c, L0_wmod):

    def _L0_attn_ref(x, w_qkv, w_out):
        import jax, jax.numpy as jnp
        import numpy as np
        N_FILTERS = 128
        N_HEADS = 16
        b, n, c = x.shape
        h = N_HEADS
        d = c // h
        qkv = jnp.einsum('bnc,ce->bne', x, w_qkv)
        q, k, v = jnp.split(qkv, 3, axis=-1)
        to_heads = lambda t: t.reshape(b, n, h, d).transpose(0, 2, 1, 3)
        q, k, v = (to_heads(q), to_heads(k), to_heads(v))
        scale = jnp.sqrt(jnp.asarray(c, jnp.float32))
        attn = jnp.einsum('bhnd,bhmd->bhnm', q, k) / scale
        attn = jax.nn.softmax(attn, axis=-1)
        out = jnp.einsum('bhnm,bhmd->bhnd', attn, v)
        out = out.transpose(0, 2, 1, 3).reshape(b, n, c)
        return jnp.einsum('bnc,co->bno', out, w_out)

    def _L0_ffn_ref(x, w_router, w_gate, w_up, w_down):
        import jax, jax.numpy as jnp
        import numpy as np
        TOP_K = 2
        EPS = 1e-20

        def _moe(x, w_router, w_gate, w_up, w_down):
            B, S, D = x.shape
            E = w_router.shape[1]
            xf = x.reshape(-1, D)
            T = xf.shape[0]
            scores = jax.nn.softmax(xf @ w_router, axis=-1)
            topk_w, topk_idx = jax.lax.top_k(scores, TOP_K)
            topk_w = topk_w / (jnp.sum(topk_w, axis=-1, keepdims=True) + EPS)
            comb = jnp.zeros((T, E), dtype=xf.dtype).at[jnp.arange(T)[:, None], topk_idx].set(topk_w)
            g = jnp.einsum('td,edh->eth', xf, w_gate)
            u = jnp.einsum('td,edh->eth', xf, w_up)
            h = jax.nn.silu(g) * u
            out_e = jnp.einsum('eth,ehd->etd', h, w_down)
            y = jnp.einsum('etd,te->td', out_e, comb)
            return y.reshape(B, S, D)
        return _moe(x, w_router, w_gate, w_up, w_down)
    x = L0_attn_x
    mod = (_silu(L0_c) @ L0_wmod).reshape(L0_c.shape[0], 6, 1, -1)
    sa, ca, ga, sb, cb, gb = (mod[:, 0], mod[:, 1], mod[:, 2], mod[:, 3], mod[:, 4], mod[:, 5])
    ga = (2 * (ga >= 0) - 1) * jnp.maximum(jnp.abs(ga), 0.25)
    gb = (2 * (gb >= 0) - 1) * jnp.maximum(jnp.abs(gb), 0.25)
    h = _layernorm(x, axis=-1) * (1 + ca) + sa
    x = x + ga * _L0_attn_ref(h, L0_attn_w_qkv, L0_attn_w_out)
    h = _layernorm(x, axis=-1) * (1 + cb) + sb
    x = x + gb * _L0_ffn_ref(h, L0_ffn_w_router, L0_ffn_w_gate, L0_ffn_w_up, L0_ffn_w_down)
    return x

_drawn_inputs = setup_inputs


def setup_inputs(seed=0):
    import zlib

    import numpy as np

    out = dict(_drawn_inputs(seed))
    spreads = {}
    factors = {'L0_attn_w_qkv': 22.25, 'L0_attn_w_out': 22.821}
    for name, (base, spread) in spreads.items():
        noise = np.random.default_rng([zlib.crc32(name.encode()), seed]).standard_normal(out[name].shape)
        drawn = base * np.exp(spread * noise) if base else spread * noise
        out[name] = jnp.asarray(drawn.astype(out[name].dtype))
    for name, factor in factors.items():
        out[name] = (out[name] * factor).astype(out[name].dtype)
    return out
```

```python
from contextlib import ExitStack

import concourse.bass as bass
from concourse import mybir

F32 = mybir.dt.float32
BF16 = mybir.dt.bfloat16
ALU = mybir.AluOpType
ACT = mybir.ActivationFunctionType
AX = mybir.AxisListType


def adaln_block(nc, x, w_qkv, w_out, w_router, w_gate, w_up, w_down, c, wmod, out):
    B, N, C = x.shape
    E, _, HID = w_gate.shape
    H = 16
    DH = C // H
    P = 128
    CH = N // P
    G = 4
    NG = H // G
    SLOTS = NG * CH
    AHEAD = SLOTS // 2
    PAIRS = H // 2
    NJ = wmod.shape[1] // C
    SA, CA, GA, SB, CB, GB = range(NJ)
    KT = E * HID // P
    KQ = 6 * DH
    KM = KQ + 3
    VW = 32
    INV_SCALE = float(C) ** -0.5
    LN_EPS, TOPK_EPS, GATE_MIN = 1e-5, 1e-20, 0.25
    Q_PARTS = (0, 0, 0, 1, 1, 2)
    K_PARTS = (0, 1, 2, 0, 1, 0)
    STACKS = 2 * 2 * len(Q_PARTS)

    TASKS = {
        (1, 0): "max1", (2, 0): "xT", (2, 1): "q", (3, 0): "k", (3, 1): "v", (4, 1): "o0", (5, 0): "max2",
        (5, 1): "o1", (6, 0): "o2", (6, 1): "o3", (7, 1): "attnT", (8, 1): "proj", (9, 0): "max3",
        (10, 1): "x1T", (11, 1): "router", (13, 0): "max0", (15, 1): "combT",
    }
    PROJECT = ("xT", "q", "k", "v")
    OUTPUT = ("o0", "o1", "o2", "o3", "attnT", "proj", "x1T", "router", "combT")
    BEFORE = PROJECT + ("max0",)

    def tasks(first, last):
        names = [TASKS[k] for k in sorted(TASKS)]
        names = [n for n in names if not (first and n in OUTPUT)]
        return [n for n in names if not (last and n in PROJECT + ("max0",))]

    SETUP_USES = 4

    def misc_use(b, first, last, name):
        if first is None:
            return SETUP_USES + BEFORE.index(name)
        base = SETUP_USES + len(BEFORE)
        if not first:
            base = base + len(tasks(True, False)) + (b - 1) * len(tasks(False, False))
        return base + tasks(first, last).index(name)

    def tail_use(n):
        return SETUP_USES + len(BEFORE) + len(tasks(True, False)) + (B - 2) * len(tasks(False, False)) \
            + len(tasks(False, True)) + n

    TAIL = OUTPUT

    ctx = ExitStack()
    with ctx:
        def sb(name, shape, dt=F32):
            return ctx.enter_context(nc.sbuf_tensor(name, shape, dt))

        def sem(name):
            return ctx.enter_context(nc.semaphore(name))

        def dram(name, shape, dt):
            return nc.dram_tensor(name, shape, dt, kind="Internal").ap()

        q_scr = dram("q_scr", (3, P, N), BF16)
        k_scr = dram("k_scr", (3, P, N), BF16)
        max_scr = dram("max_scr", (G * 3 * CH, P), BF16)

        wqkv_sb = sb("wqkv_sb", [C, 3 * C])
        wo_sb = sb("wo_sb", [C, C])
        wr_sb = sb("wr_sb", [C, E])
        wmod_sb = sb("wmod_sb", [C, NJ * C])
        c_sb = sb("c_sb", [B, C])
        c_act = sb("c_act", [B, C])
        cT = sb("cT", [C, B])
        mod = sb("mod", [C, NJ, B])
        mod_tmp = sb("mod_tmp", [C, 2, B])
        ga_rows = sb("ga_rows", [P, B, C])
        ident = sb("ident", [P, P])
        ident16 = sb("ident16", [P, P], BF16)
        neg_half = sb("neg_half", [P, CH])
        sel_e = sb("sel_e", [E, E * HID], BF16)
        sel = sb("sel", [3 * E, E * HID], BF16)
        wg_sb = sb("wg_sb", [C, E * HID])
        wu_sb = sb("wu_sb", [C, E * HID])
        wd_sb = sb("wd_sb", [P, KT, C])

        x_in = sb("x_in", [P, CH, C])
        bn1 = sb("bn1", [P, CH, 6])
        mv1 = sb("mv1", [P, CH, 2])
        ve1 = sb("ve1", [P, CH])
        rstd1 = sb("rstd1", [P, CH])
        xn = sb("xn", [P, CH, C])
        hT = sb("hT", [C, N])
        q_parts = sb("q_parts", [P, 3, N], BF16)
        k_parts = sb("k_parts", [P, 3, N], BF16)
        q_rest = sb("q_rest", [P, N])
        k_rest = sb("k_rest", [P, N])
        q_stack = [sb(f"q_stack{i}", [P, PAIRS, N], BF16) for i in range(2)]
        k_stack = [sb(f"k_stack{i}", [P, PAIRS, N], BF16) for i in range(2)]
        v_aug = [sb(f"v_aug{i}", [P, CH, H, VW]) for i in range(2)]

        negmax = [sb(f"negmax{i}", [P, G, CH]) for i in range(2)]
        negmax_rest = sb("negmax_rest", [P, G, CH])
        negmax_parts = sb("negmax_parts", [P, G, 3, CH], BF16)
        negmax_T = sb("negmax_T", [G * 3 * CH, P], BF16)
        probs = [sb(f"probs{i}", [P, G, N]) for i in range(2)]
        oT = [sb(f"oT{i}", [P, NG, N]) for i in range(2)]

        sums_inv = sb("sums_inv", [P, CH, H])
        attn = sb("attn", [P, CH, C])
        attnT = sb("attnT", [C, N])
        wo_ga = sb("wo_ga", [C, C])
        x_res = sb("x_res", [P, CH, C])
        x1 = sb("x1", [P, CH, C])
        bn2 = sb("bn2", [P, CH, 6])
        mv2 = sb("mv2", [P, CH, 2])
        ve2 = sb("ve2", [P, CH])
        rstd2 = sb("rstd2", [P, CH])
        x1n = sb("x1n", [P, CH, C])
        h2T = sb("h2T", [C, N])
        r_max = sb("r_max", [P, CH])
        r_logit = sb("r_logit", [P, CH, E])
        r_exp = sb("r_exp", [P, CH, E])
        r_sum = sb("r_sum", [P, CH])
        r_inv = sb("r_inv", [P, CH])
        r_score = sb("r_score", [P, CH, 2 * E])
        r_sorted = sb("r_sorted", [P, CH, E])
        r_top = sb("r_top", [P, CH, E])
        r_without = sb("r_without", [P, CH, 2 * E])
        r_den = sb("r_den", [P, CH])
        r_den_eps = sb("r_den_eps", [P, CH])
        r_den_inv = sb("r_den_inv", [P, CH])
        r_picked = sb("r_picked", [P, CH, E])
        comb = sb("comb", [P, CH, E])
        comb_rest = sb("comb_rest", [P, CH, E])
        comb_parts = sb("comb_parts", [P, CH, 3, E], BF16)
        combT = sb("combT", [3 * E, N], BF16)

        x1_all = sb("x1_all", [P, B, CH, C])
        h2T_all = sb("h2T_all", [C, B, N])
        combT_all = sb("combT_all", [3 * E, B, N], BF16)

        ga_tmp = probs[0][:].rearrange("p g (j c) -> p (g j) c", c=C).rearrange("p (i b) c -> p i b c", i=2)
        cT_rep = probs[1][:, 0:2, :].rearrange("p g (j c) -> p (g j) c", c=C)
        gate_act = [probs[0][:, i, :] for i in range(2)]
        gated = [probs[i][:, 3, :] for i in range(2)]
        yT = probs[0][:, 2, :]
        hidden = [probs[1][:, i, :] for i in range(2)]
        result = probs[1][:, 2, :]

        def bank(name, n=1):
            return ctx.enter_context(nc.psum_tensor(name, [P, n, N], F32))

        s_row = [bank(f"s_row{i}") for i in range(2)]
        s_col = [bank(f"s_col{i}", 2) for i in range(2)]
        o_acc = bank("o_acc")
        misc = bank("misc")
        misc_f = misc[:, 0, :]
        misc_16 = misc[:, 0, :].bitcast(BF16)
        g_ps = [s_row[0][:, 0, :], s_row[1][:, 0, :]]
        u_ps = [s_col[0][:, 0, :], s_col[0][:, 1, :]]
        c_ps = [s_col[1][:, 0, :], s_col[1][:, 1, :]]
        y_ps = o_acc[:, 0, :]
        t_ps = misc_f

        names = """
            c_loaded wqkv_loaded wo_loaded wr_loaded wmod_loaded wg_loaded wu_loaded wd_loaded
            ident_zeroed ident_ready ident16_ready half_ready sel_ones sel_cut sel_made sel_loaded consts_ready
            c_silu cT_ready rep_ready mod_raw ga_raw mod_step mod_ready
            x_loaded ln1_bn ln1_mv ln1_ve ln1_rstd xn_ready
            hT_ready q_high k_high q_rest_ready k_rest_ready q_split k_split v_ready parts_stored stacked
            misc_full misc_free row_ready row_max max_split maxT_ready max_stored max_loaded
            col_ready exp_done pv_done o_saved
            sums_ready attn_ready attnT_ready wo_ga_ready x_res_loaded x1_ready x1_kept
            ln2_bn ln2_mv ln2_ve ln2_rstd x1n_ready h2T_ready h2T_kept
            r_max_ready r_logit_ready r_exp_ready r_sum_ready r_inv_ready r_score_ready r_sorted_ready
            r_top_ready r_without_ready r_den_ready r_den_inv_ready comb_step comb_split combT_ready combT_kept
            gate_ready up_ready comb_ready gate_acted gated_ready hidden_ready down_done yT_ready
            y_back result_ready result_stored waited
        """.split()
        s = {n: sem(n) for n in names}


        block = ctx.enter_context(nc.Block())

        def over_batches(eng, body):
            body(0, 0, True, False)
            with eng.Fori(0, (B - 2) // 2) as i:
                body(2 * i + 1, 1, False, False)
                body(2 * i + 2, 0, False, False)
            body(B - 1, 1, False, True)

        def group(b, n):
            return NG * b + n

        @block.sync
        def _(sp):
            sp.dma_start(c_sb[:], c).then_inc(s["c_loaded"], 16)
            sp.dma_start(x_in[:], x[0].rearrange("(k p) c -> p k c", p=P)).then_inc(s["x_loaded"], 16)
            sp.dma_start(wmod_sb[:], wmod).then_inc(s["wmod_loaded"], 16)
            sp.dma_start(wqkv_sb[:], w_qkv).then_inc(s["wqkv_loaded"], 16)
            sp.dma_start(wo_sb[:], w_out).then_inc(s["wo_loaded"], 16)
            sp.dma_start(wr_sb[:], w_router).then_inc(s["wr_loaded"], 16)
            sp.dma_start(wg_sb[:].rearrange("d (e h) -> d e h", e=E), w_gate.rearrange("e d h -> d e h")).then_inc(s["wg_loaded"], 16)
            sp.dma_start(wu_sb[:].rearrange("d (e h) -> d e h", e=E), w_up.rearrange("e d h -> d e h")).then_inc(s["wu_loaded"], 16)
            sp.dma_start(wd_sb[:], w_down.rearrange("e h d -> (e h) d").rearrange("(k p) d -> p k d", p=P)).then_inc(s["wd_loaded"], 16)
            sp.wait_ge(s["sel_made"], 1)
            for part in range(3):
                sp.dma_start(sel[part * E:(part + 1) * E, :], sel_e[:]).then_inc(s["sel_loaded"], 16)

            def load_x(b):
                sp.wait_ge(s["xn_ready"], b)
                sp.sem_inc(s["waited"])
                sp.dma_start(x_in[:], x[bass.ds(b, 1)].rearrange("o (k p) c -> p (o k) c", p=P)).then_inc(s["x_loaded"], 16)

            def stack(b, par):
                sp.wait_ge(s["q_split"], 2 * (b + 1))
                sp.wait_ge(s["k_split"], 2 * (b + 1))
                sp.dma_start(q_scr.rearrange("t r n -> r t n"), q_parts[:]).then_inc(s["parts_stored"], 16)
                sp.dma_start(k_scr.rearrange("t r n -> r t n"), k_parts[:]).then_inc(s["parts_stored"], 16)
                sp.wait_ge(s["parts_stored"], 32 * (b + 1))
                for stack_sb, scr, parts in ((q_stack[par], q_scr, Q_PARTS), (k_stack[par], k_scr, K_PARTS)):
                    for i, part in enumerate(parts):
                        rows = scr[part].rearrange("(r a d) n -> a d r n", a=2, d=DH)
                        for a in range(2):
                            at = 64 * a + DH * i
                            sp.dma_start(stack_sb[at:at + DH, :, :], rows[a]).then_inc(s["stacked"], 16)
                sp.wait_ge(s["stacked"], 16 * STACKS * (b + 1))

            def place_max(b, par, n):
                sp.wait_ge(s["maxT_ready"], group(b, n) + 1)
                sp.dma_start(max_scr, negmax_T[:]).then_inc(s["max_stored"], 16)
                sp.wait_ge(s["max_stored"], 16 * (group(b, n) + 1))
                rows = max_scr.rearrange("(r a s k) q -> a s r (k q)", r=2, a=2, s=3)
                for a in range(2):
                    sp.dma_start(q_stack[par][64 * a + KQ:64 * a + KM, 2 * n:2 * n + 2, :], rows[a]).then_inc(s["max_loaded"], 16)
                sp.wait_ge(s["max_loaded"], 32 * (group(b, n) + 1))

            def load_res(b):
                sp.wait_ge(s["x1_ready"], b)
                sp.sem_inc(s["waited"])
                sp.dma_start(x_res[:], x[bass.ds(b, 1)].rearrange("o (k p) c -> p (o k) c", p=P)).then_inc(s["x_res_loaded"], 16)

            def keep_x1(b):
                sp.wait_ge(s["x1_ready"], b + 1)
                sp.sem_inc(s["waited"])
                sp.dma_start(x1_all[:, bass.ds(b, 1), :, :], x1[:].rearrange("p (o k) c -> p o k c", o=1)).then_inc(s["x1_kept"], 16)

            def keep_h2T(b):
                sp.wait_ge(s["h2T_ready"], b + 1)
                sp.sem_inc(s["waited"])
                sp.dma_start(h2T_all[:, bass.ds(b, 1), :], h2T[:].rearrange("p (o n) -> p o n", o=1)).then_inc(s["h2T_kept"], 16)

            def keep_combT(b):
                sp.wait_ge(s["combT_ready"], b + 2)
                sp.sem_inc(s["waited"])
                sp.dma_start(combT_all[:, bass.ds(b, 1), :], combT[:].rearrange("p (o n) -> p o n", o=1)).then_inc(s["combT_kept"], 16)

            stack(0, 0)
            place_max(0, 0, 0)

            def body(b, par, first, last):
                if not last:
                    load_x(b + 1)
                place_max(b, par, 1)
                if not last:
                    stack(b + 1, 1 - par)
                if not first:
                    load_res(b - 1)
                place_max(b, par, 2)
                if not first:
                    keep_x1(b - 1)
                place_max(b, par, 3)
                if not first:
                    keep_h2T(b - 1)
                if not last:
                    place_max(b + 1, 1 - par, 0)
                if not first:
                    keep_combT(b - 1)

            over_batches(sp, body)
            load_res(B - 1)
            keep_x1(B - 1)
            keep_h2T(B - 1)
            keep_combT(B - 1)

            with sp.Fori(0, B) as b:
                sp.wait_ge(s["result_ready"], b + 1)
                sp.sem_inc(s["waited"])
                sp.dma_start(out[bass.ds(b, 1)].rearrange("o (k p) c -> p (o k) c", p=P),
                             result.rearrange("p (k c) -> p k c", c=C)).then_inc(s["result_stored"], 16)
            sp.wait_ge(s["result_stored"], 16 * B)

        @block.gpsimd
        def _(pool):
            nc.gpsimd.memset(ident[:], 0.0).then_inc(s["ident_zeroed"], 1)
            pool.wait_ge(s["ident_zeroed"], 1)
            nc.gpsimd.affine_select(out=ident[:], in_=ident[:], compare_op=ALU.not_equal, fill=1.0, base=0,
                                    pattern=[[-1, P]], channel_multiplier=1).then_inc(s["ident_ready"], 1)
            nc.gpsimd.memset(neg_half[:], -0.5).then_inc(s["half_ready"], 1)
            nc.gpsimd.memset(sel_e[:], 1.0).then_inc(s["sel_ones"], 1)
            pool.wait_ge(s["sel_ones"], 1)
            nc.gpsimd.affine_select(out=sel_e[:], in_=sel_e[:], compare_op=ALU.is_ge, fill=0.0, base=0,
                                    pattern=[[1, E * HID]], channel_multiplier=-HID).then_inc(s["sel_cut"], 1)
            pool.wait_ge(s["sel_cut"], 1)
            nc.gpsimd.affine_select(out=sel_e[:], in_=sel_e[:], compare_op=ALU.is_ge, fill=0.0, base=HID - 1,
                                    pattern=[[-1, E * HID]], channel_multiplier=HID).then_inc(s["sel_made"], 1)
            pool.wait_ge(s["ident_ready"], 1)
            nc.gpsimd.tensor_copy(ident16[:], ident[:]).then_inc(s["ident16_ready"], 1)
            pool.wait_ge(s["half_ready"], 1)

            def rstd(b, mv, ve, out_sb, ln):
                pool.wait_ge(s[f"{ln}_mv"], b + 1)
                pool.sem_inc(s["waited"])
                nc.gpsimd.tensor_scalar(ve[:], mv[:, :, 1], LN_EPS, None, ALU.add).then_inc(s[f"{ln}_ve"], 1)
                pool.wait_ge(s[f"{ln}_ve"], b + 1)
                nc.gpsimd.tensor_tensor(out_sb[:], ve[:], neg_half[:], ALU.pow).then_inc(s[f"{ln}_rstd"], 1)

            def split_rest(b, parts, rest, given, done):
                pool.wait_ge(s[given], b + 1)
                pool.sem_inc(s["waited"])
                nc.gpsimd.tensor_copy(parts[:, 1, :], rest[:]).then_inc(s[done], 1)
                pool.wait_ge(s[done], 2 * b + 1)
                nc.gpsimd.tensor_tensor(parts[:, 2, :], rest[:], parts[:, 1, :], ALU.subtract).then_inc(s[done], 1)

            def split_max(b, n):
                k = group(b, n)
                m = negmax[n % 2]
                pool.wait_ge(s["row_max"], G * CH * (k + 1))
                if not (isinstance(b, int) and b == 0 and n == 0):
                    pool.wait_ge(s["maxT_ready"], k)
                pool.sem_inc(s["waited"])
                nc.gpsimd.tensor_copy(negmax_parts[:, :, 0, :], m[:]).then_inc(s["max_split"], 1)
                pool.wait_ge(s["max_split"], 4 * k + 1)
                nc.gpsimd.tensor_tensor(negmax_rest[:], m[:], negmax_parts[:, :, 0, :], ALU.subtract).then_inc(s["max_split"], 1)
                pool.wait_ge(s["max_split"], 4 * k + 2)
                pool.sem_inc(s["waited"])
                nc.gpsimd.tensor_copy(negmax_parts[:, :, 1, :], negmax_rest[:]).then_inc(s["max_split"], 1)
                pool.wait_ge(s["max_split"], 4 * k + 3)
                nc.gpsimd.tensor_tensor(negmax_parts[:, :, 2, :], negmax_rest[:], negmax_parts[:, :, 1, :], ALU.subtract).then_inc(s["max_split"], 1)

            def fold_ga(b):
                if not (isinstance(b, int) and b == 0):
                    pool.wait_ge(s["x1_ready"], b)
                nc.gpsimd.tensor_tensor(wo_ga[:], wo_sb[:], ga_rows[:, bass.ds(b, 1), :].rearrange("p o c -> p (o c)"), ALU.mult).then_inc(s["wo_ga_ready"], 1)

            def score(b):
                pool.wait_ge(s["r_inv_ready"], b + 1)
                nc.gpsimd.tensor_tensor(r_score[:, :, 0:E], r_exp[:], r_inv[:].unsqueeze(2).to_broadcast([P, CH, E]), ALU.mult).then_inc(s["r_score_ready"], 1)

            def denominator(b):
                pool.wait_ge(s["r_sorted_ready"], b + 1)
                nc.gpsimd.tensor_tensor(r_den[:], r_sorted[:, :, 0], r_sorted[:, :, 1], ALU.add).then_inc(s["r_den_ready"], 1)
                pool.wait_ge(s["r_den_ready"], 2 * b + 1)
                pool.sem_inc(s["waited"])
                nc.gpsimd.tensor_scalar(r_den_eps[:], r_den[:], TOPK_EPS, None, ALU.add).then_inc(s["r_den_ready"], 1)

            def combine(b):
                pool.wait_ge(s["r_without_ready"], b + 1)
                nc.gpsimd.tensor_tensor(r_picked[:], r_score[:, :, 0:E], r_without[:, :, 0:E], ALU.subtract).then_inc(s["comb_step"], 1)
                pool.wait_ge(s["comb_step"], 2 * b + 1)
                pool.wait_ge(s["r_den_inv_ready"], b + 1)
                nc.gpsimd.tensor_tensor(comb[:], r_picked[:], r_den_inv[:].unsqueeze(2).to_broadcast([P, CH, E]), ALU.mult).then_inc(s["comb_step"], 1)
                pool.wait_ge(s["comb_step"], 2 * b + 2)
                if not (isinstance(b, int) and b == 0):
                    pool.wait_ge(s["combT_ready"], b + 1)
                pool.sem_inc(s["waited"])
                nc.gpsimd.tensor_copy(comb_parts[:, :, 0, :], comb[:]).then_inc(s["comb_split"], 1)
                pool.wait_ge(s["comb_split"], 4 * b + 1)
                nc.gpsimd.tensor_tensor(comb_rest[:], comb[:], comb_parts[:, :, 0, :], ALU.subtract).then_inc(s["comb_split"], 1)
                pool.wait_ge(s["comb_split"], 4 * b + 2)
                pool.sem_inc(s["waited"])
                nc.gpsimd.tensor_copy(comb_parts[:, :, 1, :], comb_rest[:]).then_inc(s["comb_split"], 1)
                pool.wait_ge(s["comb_split"], 4 * b + 3)
                nc.gpsimd.tensor_tensor(comb_parts[:, :, 2, :], comb_rest[:], comb_parts[:, :, 1, :], ALU.subtract).then_inc(s["comb_split"], 1)

            def project(b):
                if not (isinstance(b, int) and b == 0):
                    pool.wait_ge(s["parts_stored"], 32 * b)
                split_rest(b, q_parts, q_rest, "q_rest_ready", "q_split")
                split_rest(b, k_parts, k_rest, "k_rest_ready", "k_split")

            rstd(0, mv1, ve1, rstd1, "ln1")
            project(0)
            split_max(0, 0)
            pool.wait_ge(s["mod_ready"], 2)
            pool.wait_ge(s["wo_loaded"], 16)

            def body(b, par, first, last):
                split_max(b, 1)
                if not last:
                    rstd(b + 1, mv1, ve1, rstd1, "ln1")
                    project(b + 1)
                if not first:
                    fold_ga(b - 1)
                split_max(b, 2)
                split_max(b, 3)
                if not first:
                    rstd(b - 1, mv2, ve2, rstd2, "ln2")
                    score(b - 1)
                if not last:
                    split_max(b + 1, 0)
                if not first:
                    denominator(b - 1)
                    combine(b - 1)

            over_batches(pool, body)
            fold_ga(B - 1)
            rstd(B - 1, mv2, ve2, rstd2, "ln2")
            score(B - 1)
            denominator(B - 1)
            combine(B - 1)

        @block.scalar
        def _(act):
            act.wait_ge(s["c_loaded"], 16)
            nc.scalar.activation(c_act[:], c_sb[:], ACT.Silu).then_inc(s["c_silu"], 1)

            def exp(b, t, pp):
                unit = 2 * (SLOTS * b + t) + pp
                act.wait_ge(s["col_ready"], unit + 1)
                if pp == 0 and not (isinstance(b, int) and b == 0 and t < 2):
                    act.wait_ge(s["pv_done"], SLOTS * b + t - 1)
                nc.scalar.activation(probs[t % 2][:, 2 * pp:2 * pp + 2, :], s_col[pp][:], ACT.Exp,
                                     scale=INV_SCALE).then_inc(s["exp_done"], 1)

            def save_o(b, par, n):
                act.wait_ge(s["pv_done"], SLOTS * b + CH * (n + 1))
                nc.scalar.activation(oT[par][:, n, :], o_acc[:, 0, :], ACT.Copy).then_inc(s["o_saved"], 1)

            def evacuate(use, b, par, name):
                if name == "xT":
                    act.wait_ge(s["misc_full"], use + 1)
                    nc.scalar.activation(hT[:], misc_f, ACT.Identity, scale=mod[:, CA, bass.ds(b, 1)],
                                         bias=mod[:, SA, bass.ds(b, 1)]).then_inc(s["hT_ready"], 1)
                elif name == "q":
                    act.wait_ge(s["misc_full"], use + 1)
                    if not (isinstance(b, int) and b == 0):
                        act.wait_ge(s["parts_stored"], 32 * b)
                    nc.scalar.activation(q_parts[:, 0, :], misc_f, ACT.Copy).then_inc(s["q_high"], 1)
                elif name == "k":
                    act.wait_ge(s["misc_full"], use + 1)
                    if not (isinstance(b, int) and b == 0):
                        act.wait_ge(s["parts_stored"], 32 * b)
                    nc.scalar.activation(k_parts[:, 0, :], misc_f, ACT.Copy).then_inc(s["k_high"], 1)
                elif name == "v":
                    act.wait_ge(s["misc_full"], use + 1)
                    nc.scalar.activation(v_aug[par][:, :, :, 0:DH], misc_f.rearrange("p (k h d) -> p k h d", k=CH, h=H),
                                         ACT.Copy).then_inc(s["v_ready"], 1)
                elif name.startswith("max"):
                    act.wait_ge(s["misc_full"], use + 1)
                    k = group(b, int(name[3:]))
                    if not (isinstance(b, int) and b == 0 and name == "max0"):
                        act.wait_ge(s["max_stored"], 16 * k)
                    nc.scalar.activation(negmax_T[:], misc_16[0:G * 3 * CH, 0:P], ACT.Copy).then_inc(s["maxT_ready"], 1)
                elif name == "attnT":
                    act.wait_ge(s["misc_full"], use + 1)
                    nc.scalar.activation(attnT[:], misc_f, ACT.Copy).then_inc(s["attnT_ready"], 1)
                elif name == "x1T":
                    act.wait_ge(s["misc_full"], use + 1)
                    if not (isinstance(b, int) and b == 0):
                        act.wait_ge(s["h2T_kept"], 16 * b)
                    nc.scalar.activation(h2T[:], misc_f, ACT.Identity, scale=mod[:, CB, bass.ds(b, 1)],
                                         bias=mod[:, SB, bass.ds(b, 1)]).then_inc(s["h2T_ready"], 1)
                elif name == "router":
                    act.wait_ge(s["r_logit_ready"], b + 1)
                    nc.scalar.activation(r_exp[:], r_logit[:], ACT.Exp).then_inc(s["r_exp_ready"], 1)
                elif name == "combT":
                    act.wait_ge(s["misc_full"], use + 1)
                    if not (isinstance(b, int) and b == 0):
                        act.wait_ge(s["combT_kept"], 16 * b)
                    nc.scalar.activation(combT[:], misc_16[0:3 * E, 0:N], ACT.Copy).then_inc(s["combT_ready"], 1)

            act.sem_inc(s["combT_ready"])
            act.wait_ge(s["mod_ready"], 2)
            for name in BEFORE:
                evacuate(misc_use(0, None, None, name), 0, 0, name)

            def body(b, par, first, last):
                for t in range(SLOTS):
                    for half in range(2):
                        exp(b, t, half)
                        if half == 0 and t % CH == 1 and not (first and t == 1):
                            if t == 1:
                                save_o(b - 1, 1 - par, NG - 1)
                            else:
                                save_o(b, par, t // CH - 1)
                        name = TASKS.get((t, half))
                        if name in tasks(first, last):
                            of = b + 1 if name in PROJECT + ("max0",) else b - 1 if name in OUTPUT else b
                            evacuate(misc_use(b, first, last, name), of, 1 - par if of is not b else par, name)

            over_batches(act, body)
            save_o(B - 1, 1, NG - 1)
            for n, name in enumerate(TAIL):
                evacuate(tail_use(n), B - 1, 1, name)

            def scale_y(b):
                act.wait_ge(s["down_done"], KT * (b + 1))
                if not (isinstance(b, int) and b == 0):
                    act.wait_ge(s["y_back"], b)
                nc.scalar.activation(yT, y_ps, ACT.Copy, scale=mod[:, GB, bass.ds(b, 1)]).then_inc(s["yT_ready"], 1)

            def block_body(b, first):
                for k in range(KT):
                    act.wait_ge(s["gate_ready"], KT * b + k + 1)
                    if not (first and k < 2):
                        act.wait_ge(s["gated_ready"], KT * b + k - 1)
                    nc.scalar.activation(gate_act[k % 2], g_ps[k % 2], ACT.Silu).then_inc(s["gate_acted"], 1)
                scale_y(b)

            block_body(0, True)
            with act.Fori(1, B) as b:
                block_body(b, False)

        @block.vector
        def _(dve):
            for i in range(2):
                nc.vector.memset(v_aug[i][:], 0.0).then_inc(s["consts_ready"], 1)
            dve.wait_ge(s["consts_ready"], 2)
            for i in range(2):
                nc.vector.memset(v_aug[i][:, :, :, DH], 1.0)
                nc.vector.memset(k_stack[i][32:64, :, :], 1.0)
                nc.vector.memset(k_stack[i][96:128, :, :], 1.0)
            nc.vector.memset(r_score[:, :, E:2 * E], -5.0)
            nc.vector.memset(r_top[:], -5.0).then_inc(s["consts_ready"], 1)

            def stats(b, src, bn, mv, ln):
                for k in range(CH):
                    last = nc.vector.bn_stats(bn[:, k, :], src[:, k, :])
                last.then_inc(s[f"{ln}_bn"], 1)
                dve.wait_ge(s[f"{ln}_bn"], b + 1)
                dve.sem_inc(s["waited"])
                for k in range(CH):
                    last = nc.vector.bn_aggr(mv[:, k, :], bn[:, k, :])
                last.then_inc(s[f"{ln}_mv"], 1)

            def normalise(b, src, mv, rstd, out_sb, ln, ready):
                dve.wait_ge(s[f"{ln}_rstd"], b + 1)
                for k in range(CH):
                    last = nc.vector.tensor_scalar(out_sb[:, k, :], src[:, k, :], mv[:, k, 0:1], rstd[:, k:k + 1],
                                                   ALU.subtract, ALU.mult)
                last.then_inc(s[ready], 1)

            def ln1_stats(b):
                dve.wait_ge(s["x_loaded"], 16 * (b + 1))
                stats(b, x_in, bn1, mv1, "ln1")

            def ln1_apply(b):
                normalise(b, x_in, mv1, rstd1, xn, "ln1", "xn_ready")

            def row_max(b, par, t, j):
                n, qc = t // CH, t % CH
                unit = G * (SLOTS * b + t) + j
                dve.wait_ge(s["row_ready"], unit + 1)
                if qc == 0 and j == 0 and not (isinstance(b, int) and b == 0 and n < 2):
                    dve.wait_ge(s["max_split"], 4 * (group(b, n) - 1))
                nc.vector.tensor_reduce(negmax[n % 2][:, j, qc:qc + 1], s_row[j % 2][:, 0, :], AX.X, ALU.max,
                                        negate=True).then_inc(s["row_max"], 1)

            def evacuate(use, b, par, name):
                if name == "q":
                    dve.wait_ge(s["q_high"], b + 1)
                    if not (isinstance(b, int) and b == 0):
                        dve.wait_ge(s["q_split"], 2 * b)
                    nc.vector.tensor_tensor(q_rest[:], misc_f, q_parts[:, 0, :], ALU.subtract).then_inc(s["q_rest_ready"], 1)
                elif name == "k":
                    dve.wait_ge(s["k_high"], b + 1)
                    if not (isinstance(b, int) and b == 0):
                        dve.wait_ge(s["k_split"], 2 * b)
                    nc.vector.tensor_tensor(k_rest[:], misc_f, k_parts[:, 0, :], ALU.subtract).then_inc(s["k_rest_ready"], 1)
                elif name in ("o0", "o1", "o2", "o3"):
                    k = int(name[1])
                    dve.wait_ge(s["misc_full"], use + 1)
                    o = misc_f.rearrange("p (h w) -> p h w", w=VW)
                    nc.vector.reciprocal(sums_inv[:, k, :], o[:, :, DH]).then_inc(s["sums_ready"], 1)
                    dve.wait_ge(s["sums_ready"], CH * b + k + 1)
                    nc.vector.tensor_tensor(attn[:, k, :].rearrange("p (h d) -> p h d", h=H), o[:, :, 0:DH],
                                            sums_inv[:, k, :].unsqueeze(2).to_broadcast([P, H, DH]), ALU.mult).then_inc(s["attn_ready"], 1)
                elif name == "proj":
                    dve.wait_ge(s["misc_full"], use + 1)
                    dve.wait_ge(s["x_res_loaded"], 16 * (b + 1))
                    if not (isinstance(b, int) and b == 0):
                        dve.wait_ge(s["x1_kept"], 16 * b)
                    nc.vector.tensor_tensor(x1[:].rearrange("p k c -> p (k c)"), misc_f,
                                            x_res[:].rearrange("p k c -> p (k c)"), ALU.add).then_inc(s["x1_ready"], 1)
                elif name == "router":
                    logits = misc_f[:, 0:CH * E].rearrange("p (k e) -> p k e", e=E)
                    dve.wait_ge(s["misc_full"], use + 1)
                    nc.vector.tensor_reduce(r_max[:], logits, AX.X, ALU.max).then_inc(s["r_max_ready"], 1)
                    dve.wait_ge(s["r_max_ready"], b + 1)
                    nc.vector.tensor_tensor(r_logit[:], logits, r_max[:].unsqueeze(2).to_broadcast([P, CH, E]),
                                            ALU.subtract).then_inc(s["r_logit_ready"], 1)

            def ln2_stats(b):
                dve.wait_ge(s["x1_ready"], b + 1)
                stats(b, x1, bn2, mv2, "ln2")

            def ln2_apply(b):
                normalise(b, x1, mv2, rstd2, x1n, "ln2", "x1n_ready")

            def softmax_sum(b):
                dve.wait_ge(s["r_exp_ready"], b + 1)
                nc.vector.tensor_reduce(r_sum[:], r_exp[:], AX.X, ALU.add).then_inc(s["r_sum_ready"], 1)
                dve.wait_ge(s["r_sum_ready"], b + 1)
                nc.vector.reciprocal(r_inv[:], r_sum[:]).then_inc(s["r_inv_ready"], 1)

            def pick(b):
                dve.wait_ge(s["r_score_ready"], b + 1)
                dve.sem_inc(s["waited"])
                for k in range(CH):
                    last = nc.vector.max(r_sorted[:, k, :], r_score[:, k, 0:E])
                last.then_inc(s["r_sorted_ready"], 1)
                dve.wait_ge(s["r_sorted_ready"], b + 1)
                nc.vector.tensor_copy(r_top[:, :, 0:2], r_sorted[:, :, 0:2]).then_inc(s["r_top_ready"], 1)
                dve.wait_ge(s["r_top_ready"], b + 1)
                dve.sem_inc(s["waited"])
                for k in range(CH):
                    last = nc.vector.match_replace(r_without[:, k, :], r_top[:, k, :], r_score[:, k, :], 0.0)
                last.then_inc(s["r_without_ready"], 1)

            def denominator(b):
                dve.wait_ge(s["r_den_ready"], 2 * (b + 1))
                nc.vector.reciprocal(r_den_inv[:], r_den_eps[:]).then_inc(s["r_den_inv_ready"], 1)

            dve.wait_ge(s["misc_full"], 1)
            nc.vector.tensor_copy(cT[:], misc_f[:, 0:B]).then_inc(s["cT_ready"], 1)
            dve.wait_ge(s["cT_ready"], 1)
            nc.vector.tensor_copy(cT_rep, cT[:].unsqueeze(2).to_broadcast([C, B, P])).then_inc(s["rep_ready"], 1)
            dve.wait_ge(s["misc_full"], 2)
            nc.vector.tensor_copy(mod[:].rearrange("p j b -> p (j b)"), misc_f[:, 0:NJ * B]).then_inc(s["misc_free"], 1)
            half_b = N // C
            for i in range(B // half_b):
                dve.wait_ge(s["misc_full"], 3 + i)
                nc.vector.tensor_copy(ga_rows[:, half_b * i:half_b * (i + 1), :].rearrange("p b c -> p (b c)"), misc_f).then_inc(s["misc_free"], 1)
            dve.wait_ge(s["misc_free"], 3)
            nc.vector.tensor_scalar(mod[:, CA, :], mod[:, CA, :], 1.0, None, ALU.add)
            nc.vector.tensor_scalar(mod[:, CB, :], mod[:, CB, :], 1.0, None, ALU.add)
            flat = "p b c -> p (b c)"
            for i, (g, twice, size) in enumerate((
                    (mod[:, GB, :], mod_tmp[:, 0, :], mod_tmp[:, 1, :]),
                    (ga_rows[:].rearrange(flat), ga_tmp[:, 0].rearrange(flat), ga_tmp[:, 1].rearrange(flat)))):
                nc.vector.tensor_scalar(twice, g, 0.0, 2.0, ALU.is_ge, ALU.mult).then_inc(s["mod_step"], 1)
                dve.wait_ge(s["mod_step"], 3 * i + 1)
                nc.vector.scalar_tensor_tensor(out=size, in0=twice, scalar=-1.0, in1=g, op0=ALU.add, op1=ALU.mult).then_inc(s["mod_step"], 1)
                dve.wait_ge(s["mod_step"], 3 * i + 2)
                nc.vector.tensor_scalar(size, size, GATE_MIN, None, ALU.max).then_inc(s["mod_step"], 1)
                dve.wait_ge(s["mod_step"], 3 * i + 3)
                nc.vector.scalar_tensor_tensor(out=g, in0=twice, scalar=-1.0, in1=size, op0=ALU.add, op1=ALU.mult).then_inc(s["mod_ready"], 1)

            ln1_stats(0)
            ln1_apply(0)
            for name in PROJECT:
                evacuate(misc_use(0, None, None, name), 0, 0, name)
            for t in range(AHEAD):
                for j in range(G):
                    row_max(0, 0, t, j)

            def body(b, par, first, last):
                for t in range(SLOTS):
                    for half in range(2):
                        if t < SLOTS - AHEAD:
                            for j in range(2 * half, 2 * half + 2):
                                row_max(b, par, t + AHEAD, j)
                        elif not last:
                            for j in range(2 * half, 2 * half + 2):
                                row_max(b + 1, 1 - par, t + AHEAD - SLOTS, j)
                        at = (t, half)
                        if not last:
                            if at == (1, 0):
                                ln1_stats(b + 1)
                            if at == (1, 1):
                                ln1_apply(b + 1)
                        if not first:
                            if at == (9, 0):
                                ln2_stats(b - 1)
                            if at == (10, 0):
                                ln2_apply(b - 1)
                            if at == (12, 0):
                                softmax_sum(b - 1)
                            if at == (13, 1):
                                pick(b - 1)
                            if at == (14, 1):
                                denominator(b - 1)
                        name = TASKS.get(at)
                        if name in tasks(first, last):
                            of = b + 1 if name in PROJECT + ("max0",) else b - 1 if name in OUTPUT else b
                            evacuate(misc_use(b, first, last, name), of, par, name)

            over_batches(dve, body)
            b = B - 1
            for n, name in enumerate(TAIL):
                if name == "x1T":
                    ln2_stats(b)
                    ln2_apply(b)
                if name == "combT":
                    softmax_sum(b)
                    pick(b)
                    denominator(b)
                evacuate(tail_use(n), b, 1, name)

            def store_block(b, first):
                dve.wait_ge(s["y_back"], b + 1)
                if not first:
                    dve.wait_ge(s["result_stored"], 16 * b)
                nc.vector.tensor_tensor(result, t_ps,
                                        x1_all[:, bass.ds(b, 1), :, :].rearrange("p o k c -> p (o k c)"),
                                        ALU.add).then_inc(s["result_ready"], 1)

            def block_body(b, first):
                for k in range(KT):
                    i = KT * b + k
                    dve.wait_ge(s["gate_acted"], i + 1)
                    dve.wait_ge(s["up_ready"], i + 1)
                    nc.vector.tensor_tensor(gated[k % 2], gate_act[k % 2], u_ps[k % 2], ALU.mult).then_inc(s["gated_ready"], 1)
                    dve.wait_ge(s["gated_ready"], i + 1)
                    dve.wait_ge(s["comb_ready"], i + 1)
                    if not (first and k < 2):
                        dve.wait_ge(s["down_done"], i - 1)
                    nc.vector.tensor_tensor(hidden[k % 2], gated[k % 2], c_ps[k % 2], ALU.mult).then_inc(s["hidden_ready"], 1)
                    if k == 2 and not first:
                        store_block(b - 1, False)

            dve.wait_ge(s["x1_kept"], 16 * B)
            block_body(0, True)
            with dve.Fori(1, B) as b:
                block_body(b, False)
            store_block(B - 1, False)

        @block.tensor
        def _(pe):
            pe.wait_ge(s["c_silu"], 1)
            pe.wait_ge(s["ident_ready"], 1)
            nc.tensor.transpose(misc_f[:, 0:B], c_act[:], ident[0:B, 0:B]).then_inc(s["misc_full"], 1)
            pe.wait_ge(s["cT_ready"], 1)
            pe.wait_ge(s["wmod_loaded"], 16)
            for j in range(NJ):
                last = nc.tensor.matmul(misc_f[:, B * j:B * (j + 1)], wmod_sb[:, C * j:C * (j + 1)], cT[:], start=True, stop=True)
            last.then_inc(s["misc_full"], 1)
            pe.wait_ge(s["rep_ready"], 1)
            half_b = N // C
            for i in range(B // half_b):
                pe.wait_ge(s["misc_free"], 1 + i)
                for j in range(half_b):
                    last = nc.tensor.matmul(misc_f[:, C * j:C * (j + 1)], cT_rep[:, half_b * i + j, :],
                                            wmod_sb[:, C * GA:C * (GA + 1)], start=True, stop=True)
                last.then_inc(s["misc_full"], 1)

            def free(b, name):
                if name == "xT":
                    pe.wait_ge(s["hT_ready"], b + 1)
                elif name == "q":
                    pe.wait_ge(s["q_rest_ready"], b + 1)
                elif name == "k":
                    pe.wait_ge(s["k_rest_ready"], b + 1)
                elif name == "v":
                    pe.wait_ge(s["v_ready"], b + 1)
                elif name.startswith("max"):
                    pe.wait_ge(s["maxT_ready"], group(b, int(name[3:])) + 1)
                elif name in ("o0", "o1", "o2", "o3"):
                    pe.wait_ge(s["attn_ready"], CH * b + int(name[1]) + 1)
                elif name == "attnT":
                    pe.wait_ge(s["attnT_ready"], b + 1)
                elif name == "proj":
                    pe.wait_ge(s["x1_ready"], b + 1)
                elif name == "x1T":
                    pe.wait_ge(s["h2T_ready"], b + 1)
                elif name == "router":
                    pe.wait_ge(s["r_logit_ready"], b + 1)
                elif name == "combT":
                    pe.wait_ge(s["combT_ready"], b + 2)

            def task(b, par, name):
                if name == "xT":
                    pe.wait_ge(s["xn_ready"], b + 1)
                    for k in range(CH):
                        last = nc.tensor.transpose(misc_f[:, P * k:P * (k + 1)], xn[:, k, :], ident[:])
                elif name == "q":
                    pe.wait_ge(s["wqkv_loaded"], 16)
                    last = nc.tensor.matmul(misc_f, wqkv_sb[:, 0:C], hT[:], start=True, stop=True)
                elif name == "k":
                    last = nc.tensor.matmul(misc_f, wqkv_sb[:, C:2 * C], hT[:], start=True, stop=True)
                elif name == "v":
                    for k in range(CH):
                        last = nc.tensor.matmul(misc_f[:, C * k:C * (k + 1)], hT[:, P * k:P * (k + 1)], wqkv_sb[:, 2 * C:3 * C],
                                                start=True, stop=True)
                elif name.startswith("max"):
                    pe.wait_ge(s["max_split"], 4 * (group(b, int(name[3:])) + 1))
                    pe.sem_inc(s["waited"])
                    last = nc.tensor.transpose(misc_16[0:G * 3 * CH, 0:P], negmax_parts[:].rearrange("p g s k -> p (g s k)"), ident16[:])
                elif name in ("o0", "o1", "o2", "o3"):
                    k = int(name[1])
                    for n in range(NG):
                        last = nc.tensor.transpose(misc_f[:, P * n:P * (n + 1)], oT[par][:, n, P * k:P * (k + 1)], ident[:])
                elif name == "attnT":
                    for k in range(CH):
                        last = nc.tensor.transpose(misc_f[:, P * k:P * (k + 1)], attn[:, k, :], ident[:])
                elif name == "proj":
                    pe.wait_ge(s["wo_ga_ready"], b + 1)
                    for k in range(CH):
                        last = nc.tensor.matmul(misc_f[:, C * k:C * (k + 1)], attnT[:, P * k:P * (k + 1)], wo_ga[:], start=True, stop=True)
                elif name == "x1T":
                    pe.wait_ge(s["x1n_ready"], b + 1)
                    for k in range(CH):
                        last = nc.tensor.transpose(misc_f[:, P * k:P * (k + 1)], x1n[:, k, :], ident[:])
                elif name == "router":
                    pe.wait_ge(s["wr_loaded"], 16)
                    for k in range(CH):
                        last = nc.tensor.matmul(misc_f[:, E * k:E * (k + 1)], h2T[:, P * k:P * (k + 1)], wr_sb[:], start=True, stop=True)
                elif name == "combT":
                    pe.wait_ge(s["comb_split"], 4 * (b + 1))
                    for k in range(CH):
                        last = nc.tensor.transpose(misc_16[0:3 * E, P * k:P * (k + 1)], comb_parts[:, k, :, :].rearrange("p s e -> p (s e)"), ident16[:])
                last.then_inc(s["misc_full"], 1)

            def row_scores(b, par, t, j):
                n, qc = t // CH, t % CH
                head = G * n + j
                unit = G * (SLOTS * b + t) + j
                at = 64 * (head % 2)
                if t == 0 and j == 0:
                    pe.wait_ge(s["stacked"], 16 * STACKS * (b + 1))
                if not (isinstance(b, int) and b == 0 and t == 0 and j < 2):
                    pe.wait_ge(s["row_max"], unit - 1)
                nc.tensor.matmul(s_row[j % 2][:, 0, :], q_stack[par][at:at + KQ, head // 2, P * qc:P * (qc + 1)],
                                 k_stack[par][at:at + KQ, head // 2, :], start=True, stop=True).then_inc(s["row_ready"], 1)

            def col_scores(b, par, t, pp):
                n, kc = t // CH, t % CH
                unit = 2 * (SLOTS * b + t) + pp
                pair = 2 * n + pp
                if kc == 0 and pp == 0:
                    pe.wait_ge(s["max_loaded"], 32 * (group(b, n) + 1))
                if not (isinstance(b, int) and b == 0 and t == 0):
                    pe.wait_ge(s["exp_done"], unit - 1)
                for a in range(2):
                    last = nc.tensor.matmul(s_col[pp][:, a, :], k_stack[par][64 * a:64 * a + KM, pair, P * kc:P * (kc + 1)],
                                            q_stack[par][64 * a:64 * a + KM, pair, :], start=True, stop=True)
                last.then_inc(s["col_ready"], 1)

            def weigh(b, par, t):
                n, kc = t // CH, t % CH
                pe.wait_ge(s["exp_done"], 2 * (SLOTS * b + t) + 2)
                if kc == 0 and not (isinstance(b, int) and b == 0 and n == 0):
                    pe.wait_ge(s["o_saved"], group(b, n))
                for j in range(G):
                    last = nc.tensor.matmul(o_acc[VW * j:VW * (j + 1), 0, :], v_aug[par][:, kc, G * n + j, :],
                                            probs[t % 2][:, j, :], start=(kc == 0), stop=(kc == CH - 1))
                last.then_inc(s["pv_done"], 1)

            pe.wait_ge(s["consts_ready"], 3)
            pe.wait_ge(s["ident16_ready"], 1)
            pe.wait_ge(s["misc_free"], 3)
            for i, name in enumerate(BEFORE):
                if name == "max0":
                    for t in range(AHEAD):
                        for j in range(G):
                            row_scores(0, 0, t, j)
                if i:
                    free(0, BEFORE[i - 1])
                task(0, 0, name)

            def owner(b, name):
                return b + 1 if name in PROJECT + ("max0",) else b - 1 if name in OUTPUT else b

            def body(b, par, first, last):
                mine = tasks(first, last)
                before = None
                for t in range(SLOTS):
                    for half in range(2):
                        col_scores(b, par, t, half)
                        for j in range(2 * half, 2 * half + 2):
                            if t < SLOTS - AHEAD:
                                row_scores(b, par, t + AHEAD, j)
                            elif not last:
                                row_scores(b + 1, 1 - par, t + AHEAD - SLOTS, j)
                        if half == 1:
                            if t > 0:
                                weigh(b, par, t - 1)
                            elif not first:
                                weigh(b - 1, 1 - par, SLOTS - 1)
                        name = TASKS.get((t, half))
                        if name in mine:
                            if before is not None:
                                free(owner(b, before), before)
                            elif first:
                                free(0, "max0")
                            else:
                                free(b, "max0")
                                pe.wait_ge(s["combT_ready"], b)
                            of = owner(b, name)
                            task(of, par if of is b else 1 - par, name)
                            before = name

            over_batches(pe, body)
            weigh(B - 1, 1, SLOTS - 1)
            pe.wait_ge(s["o_saved"], NG * B)
            before = "combT"
            for i, name in enumerate(TAIL):
                free(B - 2 if i == 0 else B - 1, before)
                task(B - 1, 1, name)
                before = name
            free(B - 1, "combT")

            pe.wait_ge(s["wg_loaded"], 16)
            pe.wait_ge(s["wu_loaded"], 16)
            pe.wait_ge(s["wd_loaded"], 16)
            pe.wait_ge(s["sel_loaded"], 48)
            pe.wait_ge(s["h2T_kept"], 16 * B)
            pe.wait_ge(s["combT_kept"], 16 * B)

            def down(b, k):
                pe.wait_ge(s["hidden_ready"], KT * b + k + 1)
                if k == 0 and not (isinstance(b, int) and b == 0):
                    pe.wait_ge(s["yT_ready"], b)
                nc.tensor.matmul(y_ps, wd_sb[:, k, :], hidden[k % 2], start=(k == 0), stop=(k == KT - 1)).then_inc(s["down_done"], 1)

            def block_body(b, first):
                h = h2T_all[:, bass.ds(b, 1), :].rearrange("p o n -> p (o n)")
                cw = combT_all[:, bass.ds(b, 1), :].rearrange("p o n -> p (o n)")
                for k in range(KT):
                    i = KT * b + k
                    if not (first and k < 2):
                        pe.wait_ge(s["gate_acted"], i - 1)
                    nc.tensor.matmul(g_ps[k % 2], wg_sb[:, P * k:P * (k + 1)], h, start=True, stop=True).then_inc(s["gate_ready"], 1)
                    if not (first and k < 2):
                        pe.wait_ge(s["gated_ready"], i - 1)
                    nc.tensor.matmul(u_ps[k % 2], wu_sb[:, P * k:P * (k + 1)], h, start=True, stop=True).then_inc(s["up_ready"], 1)
                    if not (first and k < 2):
                        pe.wait_ge(s["hidden_ready"], i - 1)
                        pe.sem_inc(s["waited"])
                    nc.tensor.matmul(c_ps[k % 2], sel[:, P * k:P * (k + 1)], cw, start=True, stop=True).then_inc(s["comb_ready"], 1)
                    if k == 1 and not first:
                        back(b - 1)
                    if k > 0:
                        down(b, k - 1)
                down(b, KT - 1)

            def back(b):
                pe.wait_ge(s["yT_ready"], b + 1)
                if not (isinstance(b, int) and b == 0):
                    pe.wait_ge(s["result_ready"], b)
                for k in range(CH):
                    last = nc.tensor.transpose(t_ps[:, P * k:P * (k + 1)], yT[:, P * k:P * (k + 1)], ident[:])
                last.then_inc(s["y_back"], 1)

            block_body(0, True)
            with pe.Fori(1, B) as b:
                block_body(b, False)
            back(B - 1)


_INS = ['L0_attn_x', 'L0_attn_w_qkv', 'L0_attn_w_out', 'L0_ffn_w_router', 'L0_ffn_w_gate', 'L0_ffn_w_up', 'L0_ffn_w_down', 'L0_c', 'L0_wmod']


def kernel(**inputs):
    import concourse.bacc as bacc
    import numpy as np
    from concourse.bass_utils import run_bass_kernel_spmd

    nc = bacc.Bacc("TRN2", target_bir_lowering=False, num_devices=1)
    arrays, args = {}, []
    for name in _INS:
        a = np.ascontiguousarray(inputs[name])
        arrays[f"in_{name}"] = a
        args.append(nc.dram_tensor(f"in_{name}", a.shape, mybir.dt.from_np(a.dtype), kind="ExternalInput").ap())
    out = nc.dram_tensor("out", inputs["L0_attn_x"].shape, F32, kind="ExternalOutput").ap()
    adaln_block(nc, *args, out)
    return run_bass_kernel_spmd(nc, [arrays], core_ids=[0]).results[0]["out"]
```

```python
from contextlib import ExitStack

import concourse.bass as bass
from concourse import mybir

F32 = mybir.dt.float32
F32R = mybir.dt.float32r
BF16 = mybir.dt.bfloat16
ALU = mybir.AluOpType
ACT = mybir.ActivationFunctionType
AX = mybir.AxisListType


def adaln_block(nc, x, w_qkv, w_out, w_router, w_gate, w_up, w_down, c, wmod, out):
    B, N, C = x.shape
    E, _, HID = w_gate.shape
    H = 16
    DH = C // H
    P = 128
    CH = N // P
    G = 4
    NG = H // G
    SLOTS = NG * CH
    AHEAD = 8
    NEXT_BLOCK = 2
    BACK = 5
    LAG = 3
    HIDDEN = 4
    PAIRS = H // 2
    NJ = wmod.shape[1] // C
    SA, CA, GA, SB, CB, GB = range(NJ)
    KT = E * HID // P
    KQ = 6 * DH
    KM = KQ + 3
    KS = P // 2
    VW = 32
    INV_SCALE = float(C) ** -0.5
    LN_EPS, TOPK_EPS, GATE_MIN = 1e-5, 1e-20, 0.25
    Q_RUNS = ((0, 3, 0), (1, 2, 0), (2, 1, 0))
    K_RUNS = ((0, 3, 1), (0, 2, 1), (0, 1, 1))
    STORES = 2 * len(Q_RUNS)
    LOADS = 2 * 2

    TASKS = {
        (0, 1): "max1", (1, 0): "xT", (2, 0): "q", (3, 0): "k", (4, 0): "o0", (4, 1): "max2", (5, 0): "o1", (5, 1): "o2",
        (6, 0): "o3", (6, 1): "attnT", (7, 0): "proj", (8, 1): "max3", (9, 0): "v", (11, 0): "x1T", (12, 0): "router",
        (12, 1): "max0", (15, 0): "combT",
    }
    PROJECT = ("xT", "q", "k", "v")
    NEXT = PROJECT + ("max0",)
    OUTPUT = ("o0", "o1", "o2", "o3", "attnT", "proj", "x1T", "router", "combT")
    BEFORE = NEXT

    def owner(b, name):
        return b + 1 if name in NEXT else b - 1 if name in OUTPUT else b

    def tasks(first, last):
        names = [TASKS[k] for k in sorted(TASKS)]
        names = [n for n in names if not (first and n in OUTPUT)]
        return [n for n in names if not (last and n in NEXT)]

    def misc_use(b, first, last, name):
        if first is None:
            return BEFORE.index(name)
        base = len(BEFORE)
        if not first:
            base = base + len(tasks(True, False)) + (b - 1) * len(tasks(False, False))
        return base + tasks(first, last).index(name)

    def tail_use(n):
        return len(BEFORE) + len(tasks(True, False)) + (B - 2) * len(tasks(False, False)) \
            + len(tasks(False, True)) + n

    TAIL = OUTPUT
    TAIL_AT = {0: ("o0", "o1"), 1: ("o2", "o3"), 2: ("attnT",), 3: ("proj",), 5: ("x1T",), 6: ("router",), 10: ("combT",)}

    def ring_distance(k):
        if k >= HIDDEN:
            return HIDDEN
        return k + KT - max(j for j in range(KT) if j % HIDDEN == k)

    ctx = ExitStack()
    with ctx:
        def sb(name, shape, dt=F32):
            return ctx.enter_context(nc.sbuf_tensor(name, shape, dt))

        def sem(name):
            return ctx.enter_context(nc.semaphore(name))

        def dram(name, shape, dt):
            return nc.dram_tensor(name, shape, dt, kind="Internal").ap()

        q_scr = dram("q_scr", (2, KS, PAIRS, N), BF16)
        k_scr = dram("k_scr", (2, KQ, PAIRS, N), BF16)
        max_scr = dram("max_scr", (G * 3 * CH, P), BF16)
        h2T_scr = dram("h2T_scr", (B, C, N), F32)
        combT_scr = dram("combT_scr", (B, 3 * E, N), BF16)

        wqkv_sb = sb("wqkv_sb", [C, 3 * C])
        wqk_sb = sb("wqk_sb", [C, 2, C])
        wo_sb = sb("wo_sb", [C, C])
        wr_sb = sb("wr_sb", [C, E])
        wmod_sb = sb("wmod_sb", [C, NJ * C])
        c_sb = sb("c_sb", [B, C])
        c_act = sb("c_act", [B, C])
        cT = sb("cT", [C, B])
        mod = sb("mod", [C, NJ, B])
        mod_tmp = sb("mod_tmp", [C, 2, 2, B])
        ga_rows = sb("ga_rows", [P, B, C])
        ident = sb("ident", [P, P])
        ident16 = sb("ident16", [P, P], BF16)
        neg_half = sb("neg_half", [P, (B - 1) * CH])
        sel_e = sb("sel_e", [E, E * HID], BF16)
        sel = sb("sel", [3 * E, E * HID], BF16)
        w_raw = sb("w_raw", [P, E * HID])
        wg_hi, wg_lo, wu_hi, wu_lo, wd_hi, wd_lo = (
            sb(n, [P, KT, C], F32R) for n in ("wg_hi", "wg_lo", "wu_hi", "wu_lo", "wd_hi", "wd_lo"))

        bn1 = sb("bn1", [P, B, CH, 6])
        mv1 = sb("mv1", [P, B, CH, 2])
        ve1 = sb("ve1", [P, B, CH])
        negmean1 = sb("negmean1", [P, B, CH])
        shift1 = sb("shift1", [P, B, CH])
        rstd1 = sb("rstd1", [P, B, CH])
        xn = sb("xn", [P, CH, C])
        hT = sb("hT", [C, N])
        q_parts = sb("q_parts", [P, 3, N], BF16)
        k_parts = sb("k_parts", [P, 3, N], BF16)
        q_rest = sb("q_rest", [P, N])
        k_rest = sb("k_rest", [P, N])
        q_stack = [sb(f"q_stack{i}", [P, PAIRS, N], BF16) for i in range(2)]
        k_stack = [sb(f"k_stack{i}", [P, PAIRS, N], BF16) for i in range(2)]
        v_aug = [sb(f"v_aug{i}", [P, CH, H, VW]) for i in range(2)]

        negmax = [sb(f"negmax{i}", [P, G, CH]) for i in range(2)]
        negmax_rest = sb("negmax_rest", [P, G, CH])
        negmax_parts = sb("negmax_parts", [P, G, 3, CH], BF16)
        zero_rows = sb("zero_rows", [KS - KQ, N], BF16)
        negmax_T = sb("negmax_T", [G * 3 * CH, P], BF16)
        probs = [sb(f"probs{i}", [P, G, N]) for i in range(2)]
        oT = [sb(f"oT{i}", [P, NG, N]) for i in range(2)]

        sums_inv = sb("sums_inv", [P, CH, H])
        attn = sb("attn", [P, CH, C])
        attnT = sb("attnT", [C, N])
        wo_ga = sb("wo_ga", [C, C])
        bn2 = sb("bn2", [P, CH, 6])
        mv2 = sb("mv2", [P, CH, 2])
        ve2 = sb("ve2", [P, CH])
        negmean2 = sb("negmean2", [P, CH])
        shift2 = sb("shift2", [P, CH])
        rstd2 = sb("rstd2", [P, CH])
        x1n = sb("x1n", [P, CH, C])
        h2T = sb("h2T", [C, N])
        r_max = sb("r_max", [P, CH])
        r_logit = sb("r_logit", [P, CH, E])
        r_exp = sb("r_exp", [P, CH, E])
        r_sum = sb("r_sum", [P, CH])
        r_inv = sb("r_inv", [P, CH])
        r_score = sb("r_score", [P, CH, 2 * E])
        r_sorted = sb("r_sorted", [P, CH, E])
        r_top = sb("r_top", [P, CH, E])
        r_without = sb("r_without", [P, CH, 2 * E])
        r_den = sb("r_den", [P, CH])
        r_den_eps = sb("r_den_eps", [P, CH])
        r_den_inv = sb("r_den_inv", [P, CH])
        r_picked = sb("r_picked", [P, CH, E])
        comb = sb("comb", [P, CH, E])
        comb_rest = sb("comb_rest", [P, CH, E])
        comb_parts = sb("comb_parts", [P, CH, 3, E], BF16)
        combT = sb("combT", [3 * E, N], BF16)

        x_all = sb("x_all", [P, B, CH, C])

        gate_act = [probs[0][:, i, :] for i in range(2)]
        weighed = [probs[1][:, i, :] for i in range(2)]
        yT = probs[0][:, 2, :]
        h_raw = oT[0][:, 0, :]
        result = probs[1][:, 2, :]
        gated = [probs[i][:, 3, :] for i in range(2)]
        comb_rows = sb("comb_rows", [3 * E, 2, N], BF16)
        h_hi, h_lo = ([sb(f"{n}{i}", [C, N], F32R) for i in range(2)] for n in ("h_hi", "h_lo"))
        hid_hi, hid_lo = ([sb(f"{n}{i}", [P, N], F32R) for i in range(HIDDEN)] for n in ("hid_hi", "hid_lo"))

        def bank(name, n=1):
            return ctx.enter_context(nc.psum_tensor(name, [P, n, N], F32))

        s_row = [bank(f"s_row{i}") for i in range(2)]
        s_col = [bank(f"s_col{i}", 2) for i in range(2)]
        o_acc = bank("o_acc")
        misc = bank("misc")
        misc_f = misc[:, 0, :]
        misc_16 = misc[:, 0, :].bitcast(BF16)
        g_ps = [s_row[0][:, 0, :], s_row[1][:, 0, :]]
        u_ps = [s_col[0][:, 0, :], s_col[0][:, 1, :]]
        c_ps = [s_col[1][:, 0, :], s_col[1][:, 1, :]]
        y_ps = o_acc[:, 0, :]

        names = """
            c_loaded wqkv_loaded wo_loaded wr_loaded wmod_loaded w_loaded x0_loaded x_loaded
            ident_zeroed ident_ready ident16_ready half_ready sel_ones sel_cut sel_made sel_loaded
            v_zeroed v_const stack_ones rows_zeroed zeros_stored top_const wqk_ready
            c_silu cT_ready mod_full mod_step mod_ready w_high w_split
            ln1_bn ln1_mv ln1_step ln1_ready xn_ready
            hT_ready q_high k_high q_rest_ready k_rest_ready q_mid k_mid q_split k_split v_ready
            q_stored k_stored stacked
            misc_full row_ready row_max max_split maxT_ready max_stored max_loaded
            col_ready exp_done pv_done o_saved
            sums_ready attn_ready attnT_ready wo_ga_ready x1_ready
            ln2_bn ln2_mv ln2_step ln2_ready x1n_ready h2T_ready h2T_kept
            r_max_ready r_logit_ready r_exp_ready r_sum_ready r_inv_ready r_score_ready r_sorted_ready
            r_top_ready r_without_ready r_den_ready r_den_inv_ready comb_step comb_split combT_ready combT_kept
            h_loaded comb_loaded0 comb_loaded1 h_high h_split gate_ready up_ready comb_ready gate_acted gated_ready weighed_ready
            hid_high hid_split down_done yT_ready y_back result_ready result_stored waited
        """.split()
        s = {n: sem(n) for n in names}


        block = ctx.enter_context(nc.Block())

        def over_batches(eng, body):
            body(0, 0, True, False)
            with eng.Fori(0, (B - 2) // 2) as i:
                body(2 * i + 1, 1, False, False)
                body(2 * i + 2, 0, False, False)
            body(B - 1, 1, False, True)

        def group(b, n):
            return NG * b + n

        @block.sync
        def _(sp):
            by_rows = "b (k p) c -> p b k c"
            sp.dma_start(x_all[:, 0:1, :, :], x[0:1].rearrange(by_rows, p=P)).then_inc(s["x0_loaded"], 16)
            sp.dma_start(c_sb[:], c).then_inc(s["c_loaded"], 16)
            sp.dma_start(wmod_sb[:], wmod).then_inc(s["wmod_loaded"], 16)
            sp.dma_start(wqkv_sb[:], w_qkv).then_inc(s["wqkv_loaded"], 16)
            sp.dma_start(x_all[:, 1:B, :, :], x[1:B].rearrange(by_rows, p=P)).then_inc(s["x_loaded"], 16)
            sp.dma_start(wo_sb[:], w_out).then_inc(s["wo_loaded"], 16)
            sp.dma_start(wr_sb[:], w_router).then_inc(s["wr_loaded"], 16)

            def store_parts(b, parts_sb, scr, runs, split, stored):
                sp.wait_ge(s[split], b + 1)
                at = 0
                for part, n, step in runs:
                    for a in range(2):
                        src = parts_sb[64 * a:64 * a + 64, part:part + (n if step else 1), :]
                        if not step:
                            src = src.to_broadcast([64, n, N])
                        sp.dma_start(scr[a, DH * at:DH * (at + n)].rearrange("(t d) r n -> (d r) t n", d=DH), src).then_inc(s[stored], 16)
                    at += n

            def load_stacks(b, par):
                if isinstance(b, int) and b < 2:
                    sp.wait_ge(s["zeros_stored"], 32)
                    sp.wait_ge(s["stack_ones"], b + 1)
                for stack_sb, scr, stored, rows in ((q_stack[par], q_scr, "q_stored", KS), (k_stack[par], k_scr, "k_stored", KQ)):
                    sp.wait_ge(s[stored], 16 * STORES * (b + 1))
                    for a in range(2):
                        sp.dma_start(stack_sb[64 * a:64 * a + rows, :, :], scr[a]).then_inc(s["stacked"], 16)

            def stack(b, par):
                if not (isinstance(b, int) and b == 0):
                    sp.wait_ge(s["stacked"], 16 * LOADS * b)
                    sp.sem_inc(s["waited"])
                store_parts(b, q_parts, q_scr, Q_RUNS, "q_split", "q_stored")
                store_parts(b, k_parts, k_scr, K_RUNS, "k_split", "k_stored")
                load_stacks(b, par)

            def keep_h2T(b):
                sp.wait_ge(s["h2T_ready"], b + 1)
                sp.sem_inc(s["waited"])
                sp.dma_start(h2T_scr[bass.ds(b, 1)].rearrange("o c n -> c (o n)"), h2T[:]).then_inc(s["h2T_kept"], 16)

            def keep_combT(b):
                sp.wait_ge(s["combT_ready"], b + 2)
                sp.sem_inc(s["waited"])
                sp.dma_start(combT_scr[bass.ds(b, 1)].rearrange("o e n -> e (o n)"), combT[:]).then_inc(s["combT_kept"], 16)

            sp.wait_ge(s["rows_zeroed"], 1)
            for a in range(2):
                sp.dma_start(q_scr[a, KQ:KS], zero_rows[:].unsqueeze(1).to_broadcast([KS - KQ, PAIRS, N])).then_inc(s["zeros_stored"], 16)
            stack(0, 0)

            def load_weights(i):
                if i:
                    sp.wait_ge(s["w_split"], i)
                if i < 2:
                    sp.dma_start(w_raw[:].rearrange("d (e h) -> d e h", e=E), (w_gate, w_up)[i].rearrange("e d h -> d e h")).then_inc(s["w_loaded"], 16)
                else:
                    sp.dma_start(w_raw[:].rearrange("p (k d) -> p k d", k=KT),
                                 w_down.rearrange("e h d -> (e h) d").rearrange("(k p) d -> p k d", p=P)).then_inc(s["w_loaded"], 16)

            def body(b, par, first, last):
                if not last:
                    stack(b + 1, 1 - par)
                if first:
                    for i in range(3):
                        load_weights(i)
                    sp.wait_ge(s["sel_made"], 1)
                    for part in range(3):
                        sp.dma_start(sel[part * E:(part + 1) * E, :], sel_e[:]).then_inc(s["sel_loaded"], 16)
                if not first:
                    keep_h2T(b - 1)
                    keep_combT(b - 1)

            over_batches(sp, body)

            def fetch_h(b):
                if isinstance(b, int) and b == 0:
                    sp.wait_ge(s["o_saved"], NG * B)
                    sp.wait_ge(s["h2T_kept"], 16 * (B - 1))
                else:
                    if isinstance(b, int) and b == B - 1:
                        sp.wait_ge(s["h2T_kept"], 16 * B)
                    sp.wait_ge(s["h_split"], b)
                sp.sem_inc(s["waited"])
                sp.dma_start(h_raw, h2T_scr[bass.ds(b, 1)].rearrange("o c n -> c (o n)")).then_inc(s["h_loaded"], 16)

            def fetch_comb(b, par):
                if isinstance(b, int) and b < 2:
                    sp.wait_ge(s["combT_kept"], 16 * (b + 1))
                else:
                    if isinstance(b, int) and b == B - 1:
                        sp.wait_ge(s["combT_kept"], 16 * B)
                    sp.wait_ge(s["comb_ready"], KT * (b - 1))
                sp.sem_inc(s["waited"])
                sp.dma_start(comb_rows[:, par, :], combT_scr[bass.ds(b, 1)].rearrange("o e n -> e (o n)")).then_inc(s[f"comb_loaded{par}"], 16)

            def store_result(b):
                sp.wait_ge(s["result_ready"], b + 1)
                sp.sem_inc(s["waited"])
                sp.dma_start(out[bass.ds(b, 1)].rearrange("o (k p) c -> p (o k) c", p=P),
                             result.rearrange("p (k c) -> p k c", c=C)).then_inc(s["result_stored"], 16)

            def block_body(b, par):
                fetch_h(b + 2)
                fetch_comb(b + 2, par)
                store_result(b)

            for b in range(2):
                fetch_h(b)
                fetch_comb(b, b)
            keep_h2T(B - 1)
            fetch_h(2)
            keep_combT(B - 1)
            fetch_comb(2, 0)
            store_result(0)
            with sp.Fori(0, (B - 4) // 2) as i:
                block_body(2 * i + 1, 1)
                block_body(2 * i + 2, 0)
            block_body(B - 3, 1)
            store_result(B - 2)
            store_result(B - 1)
            sp.wait_ge(s["result_stored"], 16 * B)

        @block.gpsimd
        def _(pool):
            nc.gpsimd.memset(ident[:], 0.0).then_inc(s["ident_zeroed"], 1)
            pool.wait_ge(s["ident_zeroed"], 1)
            nc.gpsimd.affine_select(out=ident[:], in_=ident[:], compare_op=ALU.not_equal, fill=1.0, base=0,
                                    pattern=[[-1, P]], channel_multiplier=1).then_inc(s["ident_ready"], 1)
            nc.gpsimd.memset(zero_rows[:], 0.0).then_inc(s["rows_zeroed"], 1)
            nc.gpsimd.memset(neg_half[:], -0.5).then_inc(s["half_ready"], 1)

            def constants(par):
                nc.gpsimd.memset(k_stack[par][:], 1.0).then_inc(s["stack_ones"], 1)
                nc.gpsimd.memset(v_aug[par][:], 0.0).then_inc(s["v_zeroed"], 1)
                pool.wait_ge(s["v_zeroed"], par + 1)
                nc.gpsimd.memset(v_aug[par][:, :, :, DH], 1.0).then_inc(s["v_const"], 1)

            def selector():
                nc.gpsimd.memset(sel_e[:], 1.0).then_inc(s["sel_ones"], 1)
                pool.wait_ge(s["sel_ones"], 1)
                nc.gpsimd.affine_select(out=sel_e[:], in_=sel_e[:], compare_op=ALU.is_ge, fill=0.0, base=0,
                                        pattern=[[1, E * HID]], channel_multiplier=-HID).then_inc(s["sel_cut"], 1)
                pool.wait_ge(s["sel_cut"], 1)
                nc.gpsimd.affine_select(out=sel_e[:], in_=sel_e[:], compare_op=ALU.is_ge, fill=0.0, base=HID - 1,
                                        pattern=[[-1, E * HID]], channel_multiplier=HID).then_inc(s["sel_made"], 1)

            def ln_factors(n, mv, ve, negmean, rstd, shift, ln):
                pool.wait_ge(s[f"{ln}_mv"], n + 1)
                pool.sem_inc(s["waited"])
                nc.gpsimd.tensor_scalar(ve, mv[:, :, 1], LN_EPS, None, ALU.add)
                nc.gpsimd.tensor_scalar(negmean, mv[:, :, 0], -1.0, None, ALU.mult).then_inc(s[f"{ln}_step"], 1)
                pool.wait_ge(s[f"{ln}_step"], 2 * n + 1)
                nc.gpsimd.tensor_tensor(rstd, ve, neg_half[:, 0:rstd.shape[1]], ALU.pow).then_inc(s[f"{ln}_step"], 1)
                pool.wait_ge(s[f"{ln}_step"], 2 * n + 2)
                nc.gpsimd.tensor_tensor(shift, negmean, rstd, ALU.mult).then_inc(s[f"{ln}_ready"], 1)

            def ln1_factors(n, b0, b1):
                flat = "p b k -> p (b k)"
                ln_factors(n, mv1[:, b0:b1].rearrange("p b k m -> p (b k) m"), ve1[:, b0:b1].rearrange(flat), negmean1[:, b0:b1].rearrange(flat),
                           rstd1[:, b0:b1].rearrange(flat), shift1[:, b0:b1].rearrange(flat), "ln1")

            def low_part(b, parts, rest, mid, done):
                pool.wait_ge(s[mid], b + 1)
                nc.gpsimd.tensor_tensor(parts[:, 2, :], rest[:], parts[:, 1, :], ALU.subtract).then_inc(s[done], 1)

            def split_weights(i):
                pool.wait_ge(s["w_high"], i + 1)
                nc.gpsimd.tensor_tensor((wg_lo, wu_lo, wd_lo)[i][:].rearrange("p k c -> p (k c)"), w_raw[:],
                                        (wg_hi, wu_hi, wd_hi)[i][:].rearrange("p k c -> p (k c)"), ALU.subtract).then_inc(s["w_split"], 1)

            def split_max(b, n):
                k = group(b, n)
                m = negmax[n % 2]
                pool.wait_ge(s["row_max"], G * CH * (k + 1))
                if not (isinstance(b, int) and b == 0 and n == 0):
                    pool.wait_ge(s["maxT_ready"], k)
                pool.sem_inc(s["waited"])
                nc.gpsimd.tensor_copy(negmax_parts[:, :, 0, :], m[:]).then_inc(s["max_split"], 1)
                pool.wait_ge(s["max_split"], 4 * k + 1)
                nc.gpsimd.tensor_tensor(negmax_rest[:], m[:], negmax_parts[:, :, 0, :], ALU.subtract).then_inc(s["max_split"], 1)
                pool.wait_ge(s["max_split"], 4 * k + 2)
                pool.sem_inc(s["waited"])
                nc.gpsimd.tensor_copy(negmax_parts[:, :, 1, :], negmax_rest[:]).then_inc(s["max_split"], 1)
                pool.wait_ge(s["max_split"], 4 * k + 3)
                nc.gpsimd.tensor_tensor(negmax_parts[:, :, 2, :], negmax_rest[:], negmax_parts[:, :, 1, :], ALU.subtract).then_inc(s["max_split"], 1)

            def fold_ga(b):
                if not (isinstance(b, int) and b == 0):
                    pool.wait_ge(s["x1_ready"], b)
                nc.gpsimd.tensor_tensor(wo_ga[:], wo_sb[:], ga_rows[:, bass.ds(b, 1), :].rearrange("p o c -> p (o c)"), ALU.mult).then_inc(s["wo_ga_ready"], 1)

            def score(b):
                pool.wait_ge(s["r_inv_ready"], b + 1)
                nc.gpsimd.tensor_tensor(r_score[:, :, 0:E], r_exp[:], r_inv[:].unsqueeze(2).to_broadcast([P, CH, E]), ALU.mult).then_inc(s["r_score_ready"], 1)

            def denominator(b):
                pool.wait_ge(s["r_sorted_ready"], b + 1)
                nc.gpsimd.tensor_tensor(r_den[:], r_sorted[:, :, 0], r_sorted[:, :, 1], ALU.add).then_inc(s["r_den_ready"], 1)
                pool.wait_ge(s["r_den_ready"], 2 * b + 1)
                pool.sem_inc(s["waited"])
                nc.gpsimd.tensor_scalar(r_den_eps[:], r_den[:], TOPK_EPS, None, ALU.add).then_inc(s["r_den_ready"], 1)

            def combine(b):
                pool.wait_ge(s["r_without_ready"], b + 1)
                nc.gpsimd.tensor_tensor(r_picked[:], r_score[:, :, 0:E], r_without[:, :, 0:E], ALU.subtract).then_inc(s["comb_step"], 1)
                pool.wait_ge(s["comb_step"], 2 * b + 1)
                pool.wait_ge(s["r_den_inv_ready"], b + 1)
                nc.gpsimd.tensor_tensor(comb[:], r_picked[:], r_den_inv[:].unsqueeze(2).to_broadcast([P, CH, E]), ALU.mult).then_inc(s["comb_step"], 1)
                pool.wait_ge(s["comb_step"], 2 * b + 2)
                if not (isinstance(b, int) and b == 0):
                    pool.wait_ge(s["combT_ready"], b + 1)
                pool.sem_inc(s["waited"])
                nc.gpsimd.tensor_copy(comb_parts[:, :, 0, :], comb[:]).then_inc(s["comb_split"], 1)
                pool.wait_ge(s["comb_split"], 4 * b + 1)
                nc.gpsimd.tensor_tensor(comb_rest[:], comb[:], comb_parts[:, :, 0, :], ALU.subtract).then_inc(s["comb_split"], 1)
                pool.wait_ge(s["comb_split"], 4 * b + 2)
                pool.sem_inc(s["waited"])
                nc.gpsimd.tensor_copy(comb_parts[:, :, 1, :], comb_rest[:]).then_inc(s["comb_split"], 1)
                pool.wait_ge(s["comb_split"], 4 * b + 3)
                nc.gpsimd.tensor_tensor(comb_parts[:, :, 2, :], comb_rest[:], comb_parts[:, :, 1, :], ALU.subtract).then_inc(s["comb_split"], 1)

            def project(b):
                low_part(b, q_parts, q_rest, "q_mid", "q_split")
                low_part(b, k_parts, k_rest, "k_mid", "k_split")

            pool.wait_ge(s["half_ready"], 1)
            ln1_factors(0, 0, 1)
            pool.wait_ge(s["ident_ready"], 1)
            nc.gpsimd.tensor_copy(ident16[:], ident[:]).then_inc(s["ident16_ready"], 1)
            constants(0)
            project(0)
            ln1_factors(1, 1, B)
            constants(1)
            nc.gpsimd.memset(r_score[:, :, E:2 * E], -5.0)
            nc.gpsimd.memset(r_top[:], -5.0).then_inc(s["top_const"], 1)
            split_max(0, 0)
            selector()
            pool.wait_ge(s["mod_ready"], 3)
            pool.wait_ge(s["wo_loaded"], 16)

            def body(b, par, first, last):
                split_max(b, 1)
                if not last:
                    project(b + 1)
                if not first:
                    fold_ga(b - 1)
                split_max(b, 2)
                if first:
                    split_weights(0)
                split_max(b, 3)
                if first:
                    split_weights(1)
                else:
                    ln_factors(b - 1, mv2[:], ve2[:], negmean2[:], rstd2[:], shift2[:], "ln2")
                if not last:
                    split_max(b + 1, 0)
                if first:
                    split_weights(2)
                else:
                    score(b - 1)
                    denominator(b - 1)
                    combine(b - 1)

            over_batches(pool, body)

            def hid_low(b, par, k):
                pool.wait_ge(s["hid_high"], KT * b + k + 1)
                nc.gpsimd.tensor_tensor(hid_lo[k % HIDDEN][:], weighed[(par + k) % 2], hid_hi[k % HIDDEN][:], ALU.subtract).then_inc(s["hid_split"], 1)

            def block_low(b, par):
                pool.wait_ge(s["h_high"], b + 1)
                pool.sem_inc(s["waited"])
                nc.gpsimd.tensor_tensor(h_lo[par][:], h_raw, h_hi[par][:],
                                        ALU.subtract).then_inc(s["h_split"], 1)

            def block_body(b, par, first, last):
                for k in range(KT):
                    if first:
                        if k == 0:
                            fold_ga(B - 1)
                        elif k == 4:
                            ln_factors(B - 1, mv2[:], ve2[:], negmean2[:], rstd2[:], shift2[:], "ln2")
                        elif k == 8:
                            score(B - 1)
                            denominator(B - 1)
                            combine(B - 1)
                    if k == NEXT_BLOCK and not last:
                        block_low(b + 1, 1 - par)
                    hid_low(b, par, k)

            block_low(0, 0)
            over_batches(pool, block_body)

        @block.scalar
        def _(act):
            act.wait_ge(s["c_loaded"], 16)
            nc.scalar.activation(c_act[:], c_sb[:], ACT.Silu).then_inc(s["c_silu"], 1)

            def normalise(b, out_sb, rstd, shift, ready):
                for k in range(CH):
                    last = nc.scalar.activation(out_sb[:, k, :], x_all[:, bass.ds(b, 1), k, :].rearrange("p o c -> p (o c)"),
                                                ACT.Identity, scale=rstd(k), bias=shift(k))
                last.then_inc(s[ready], 1)

            def normalise1(b):
                normalise(b, xn, lambda k: rstd1[:, bass.ds(b, 1), k], lambda k: shift1[:, bass.ds(b, 1), k], "xn_ready")

            def normalise2(b):
                act.wait_ge(s["ln2_ready"], b + 1)
                normalise(b, x1n, lambda k: rstd2[:, k:k + 1], lambda k: shift2[:, k:k + 1], "x1n_ready")

            def exp(b, t, pp):
                unit = 2 * (SLOTS * b + t) + pp
                act.wait_ge(s["col_ready"], unit + 1)
                if pp == 0 and not (isinstance(b, int) and b == 0 and t < 2):
                    act.wait_ge(s["pv_done"], SLOTS * b + t - 1)
                nc.scalar.activation(probs[t % 2][:, 2 * pp:2 * pp + 2, :], s_col[pp][:], ACT.Exp,
                                     scale=INV_SCALE).then_inc(s["exp_done"], 1)

            def save_o(b, par, n):
                act.wait_ge(s["pv_done"], SLOTS * b + CH * (n + 1))
                nc.scalar.activation(oT[par][:, n, :], o_acc[:, 0, :], ACT.Copy).then_inc(s["o_saved"], 1)

            def middle_part(b, parts, rest, rest_ready, mid):
                act.wait_ge(s[rest_ready], b + 1)
                nc.scalar.activation(parts[:, 1, :], rest[:], ACT.Copy).then_inc(s[mid], 1)

            def store_max(b, n):
                act.wait_ge(s["maxT_ready"], group(b, n) + 1)
                nc.scalar.dma_start(max_scr, negmax_T[:]).then_inc(s["max_stored"], 16)

            def place_max(b, par, n):
                act.wait_ge(s["max_stored"], 16 * (group(b, n) + 1))
                rows = max_scr.rearrange("(r a s k) q -> a s r (k q)", r=2, a=2, s=3)
                for a in range(2):
                    nc.scalar.dma_start(q_stack[par][64 * a + KQ:64 * a + KM, 2 * n:2 * n + 2, :], rows[a]).then_inc(s["max_loaded"], 16)

            def evacuate(use, b, par, name):
                if name == "xT":
                    act.wait_ge(s["misc_full"], use + 1)
                    nc.scalar.activation(hT[:], misc_f, ACT.Identity, scale=mod[:, CA, bass.ds(b, 1)],
                                         bias=mod[:, SA, bass.ds(b, 1)]).then_inc(s["hT_ready"], 1)
                elif name == "q":
                    act.wait_ge(s["misc_full"], use + 1)
                    if not (isinstance(b, int) and b == 0):
                        act.wait_ge(s["q_stored"], 16 * STORES * b)
                    nc.scalar.activation(q_parts[:, 0, :], misc_f, ACT.Copy).then_inc(s["q_high"], 1)
                elif name == "k":
                    middle_part(b, q_parts, q_rest, "q_rest_ready", "q_mid")
                    act.wait_ge(s["misc_full"], use + 1)
                    if not (isinstance(b, int) and b == 0):
                        act.wait_ge(s["k_stored"], 16 * STORES * b)
                    nc.scalar.activation(k_parts[:, 0, :], misc_f, ACT.Copy).then_inc(s["k_high"], 1)
                elif name == "v":
                    act.wait_ge(s["misc_full"], use + 1)
                    nc.scalar.activation(v_aug[par][:, :, :, 0:DH], misc_f.rearrange("p (k h d) -> p k h d", k=CH, h=H),
                                         ACT.Copy).then_inc(s["v_ready"], 1)
                elif name.startswith("max"):
                    act.wait_ge(s["misc_full"], use + 1)
                    k = group(b, int(name[3:]))
                    if not (isinstance(b, int) and b == 0 and name == "max0"):
                        act.wait_ge(s["max_loaded"], 32 * k)
                    nc.scalar.activation(negmax_T[:], misc_16[0:G * 3 * CH, 0:P], ACT.Copy).then_inc(s["maxT_ready"], 1)
                elif name == "attnT":
                    act.wait_ge(s["misc_full"], use + 1)
                    nc.scalar.activation(attnT[:], misc_f, ACT.Copy).then_inc(s["attnT_ready"], 1)
                elif name == "x1T":
                    act.wait_ge(s["misc_full"], use + 1)
                    if not (isinstance(b, int) and b == 0):
                        act.wait_ge(s["h2T_kept"], 16 * b)
                    nc.scalar.activation(h2T[:], misc_f, ACT.Identity, scale=mod[:, CB, bass.ds(b, 1)],
                                         bias=mod[:, SB, bass.ds(b, 1)]).then_inc(s["h2T_ready"], 1)
                elif name == "router":
                    act.wait_ge(s["r_logit_ready"], b + 1)
                    nc.scalar.activation(r_exp[:], r_logit[:], ACT.Exp).then_inc(s["r_exp_ready"], 1)
                elif name == "combT":
                    act.wait_ge(s["misc_full"], use + 1)
                    if not (isinstance(b, int) and b == 0):
                        act.wait_ge(s["combT_kept"], 16 * b)
                    nc.scalar.activation(combT[:], misc_16[0:3 * E, 0:N], ACT.Copy).then_inc(s["combT_ready"], 1)

            def split_weights(i):
                act.wait_ge(s["w_loaded"], 16 * (i + 1))
                nc.scalar.activation((wg_hi, wu_hi, wd_hi)[i][:].rearrange("p k c -> p (k c)"), w_raw[:], ACT.Copy).then_inc(s["w_high"], 1)

            act.sem_inc(s["combT_ready"])
            act.wait_ge(s["ln1_ready"], 1)
            normalise1(0)
            act.wait_ge(s["mod_ready"], 1)
            act.wait_ge(s["v_const"], 1)
            for name in BEFORE:
                if name == "v":
                    middle_part(0, k_parts, k_rest, "k_rest_ready", "k_mid")
                evacuate(misc_use(0, None, None, name), 0, 0, name)
                if name.startswith("max"):
                    store_max(0, int(name[3:]))
                    place_max(0, 0, int(name[3:]))

            NORMALISE_1, NORMALISE_2, MIDDLE_K = (0, 0), (10, 1), (4, 0)
            STORE_MAX = {(1, 0): 1, (5, 0): 2, (9, 0): 3, (13, 0): 0}
            PLACE_MAX = {(2, 0): 1, (6, 0): 2, (10, 0): 3, (14, 0): 0}
            SPLIT_WEIGHTS = {(5, 1): 0, (8, 1): 1, (12, 1): 2}

            def body(b, par, first, last):
                for t in range(SLOTS):
                    for half in range(2):
                        at = (t, half)
                        exp(b, t, half)
                        if half == 0 and t % CH == 1 and not (first and t == 1):
                            if t == 1:
                                save_o(b - 1, 1 - par, NG - 1)
                            else:
                                save_o(b, par, t // CH - 1)
                        for table, step in ((STORE_MAX, store_max), (PLACE_MAX, place_max)):
                            n = table.get(at)
                            if n is None or (n == 0 and last):
                                continue
                            of, of_par = (b + 1, 1 - par) if n == 0 else (b, par)
                            if step is store_max:
                                step(of, n)
                            else:
                                step(of, of_par, n)
                        if at == NORMALISE_1 and not last:
                            if first:
                                act.wait_ge(s["v_const"], 2)
                                act.wait_ge(s["ln1_ready"], 2)
                            normalise1(b + 1)
                        if at == MIDDLE_K and not last:
                            middle_part(b + 1, k_parts, k_rest, "k_rest_ready", "k_mid")
                        if at == NORMALISE_2 and not first:
                            normalise2(b - 1)
                        if first and at in SPLIT_WEIGHTS:
                            split_weights(SPLIT_WEIGHTS[at])
                        name = TASKS.get(at)
                        if name in tasks(first, last):
                            of = owner(b, name)
                            evacuate(misc_use(b, first, last, name), of, 1 - par if of is not b else par, name)

            over_batches(act, body)
            save_o(B - 1, 1, NG - 1)

            def block_high(b, par):
                act.wait_ge(s["h_loaded"], 16 * (b + 1))
                nc.scalar.activation(h_hi[par][:], h_raw, ACT.Copy).then_inc(s["h_high"], 1)

            def hid_high(b, par, k, wait_ring):
                i = KT * b + k
                act.wait_ge(s["weighed_ready"], i + 1)
                if wait_ring:
                    act.wait_ge(s["down_done"], i + 1 - ring_distance(k))
                nc.scalar.activation(hid_hi[k % HIDDEN][:], weighed[(par + k) % 2], ACT.Copy).then_inc(s["hid_high"], 1)

            def scale_y(b):
                act.wait_ge(s["down_done"], KT * (b + 1))
                if not (isinstance(b, int) and b == 0):
                    act.wait_ge(s["y_back"], b)
                nc.scalar.activation(yT, y_ps, ACT.Copy, scale=mod[:, GB, bass.ds(b, 1)]).then_inc(s["yT_ready"], 1)

            def block_body(b, par, first, last):
                for k in range(KT):
                    i = KT * b + k
                    if k == LAG and not first:
                        scale_y(b - 1)
                    act.wait_ge(s["gate_ready"], i + 1)
                    if not (first and k < 2):
                        act.wait_ge(s["gated_ready"], i - 1)
                    nc.scalar.activation(gate_act[(par + k) % 2], g_ps[(par + k) % 2], ACT.Silu).then_inc(s["gate_acted"], 1)
                    if k:
                        hid_high(b, par, k - 1, not (first and k - 1 < HIDDEN))
                    elif not first:
                        hid_high(b - 1, 1 - par, KT - 1, True)
                    if k == NEXT_BLOCK and not last:
                        block_high(b + 1, 1 - par)
                    if first:
                        if k == 4:
                            normalise2(B - 1)
                        for name in TAIL_AT.get(k, ()):
                            evacuate(tail_use(TAIL.index(name)), B - 1, 1, name)

            block_high(0, 0)
            over_batches(act, block_body)
            hid_high(B - 1, 1, KT - 1, True)
            scale_y(B - 1)

        @block.vector
        def _(dve):
            def bn_stats(b, bn, k):
                return nc.vector.bn_stats(bn[:, k, :], x_all[:, bass.ds(b, 1), k, :].rearrange("p o c -> p (o c)"))

            def bn_aggregate(b, bn, mv, bn_done):
                dve.wait_ge(s[bn_done], b + 1)
                dve.sem_inc(s["waited"])
                for k in range(CH):
                    last = nc.vector.bn_aggr(mv[:, k, :], bn[:, k, :])
                return last

            def ln1_stats(b):
                for k in range(CH):
                    last = bn_stats(b, bn1[:, b], k)
                last.then_inc(s["ln1_bn"], 1)
                last = bn_aggregate(b, bn1[:, b], mv1[:, b], "ln1_bn")
                if b in (0, B - 1):
                    last.then_inc(s["ln1_mv"], 1)

            def row_max(b, par, t, j):
                n, qc = t // CH, t % CH
                unit = G * (SLOTS * b + t) + j
                dve.wait_ge(s["row_ready"], unit + 1)
                if qc == 0 and j == 0 and not (isinstance(b, int) and b == 0 and n < 2):
                    dve.wait_ge(s["max_split"], 4 * (group(b, n) - 1))
                nc.vector.tensor_reduce(negmax[n % 2][:, j, qc:qc + 1], s_row[j % 2][:, 0, :], AX.X, ALU.max,
                                        negate=True).then_inc(s["row_max"], 1)

            def evacuate(use, b, par, name):
                if name == "q":
                    dve.wait_ge(s["q_high"], b + 1)
                    if not (isinstance(b, int) and b == 0):
                        dve.wait_ge(s["q_split"], b)
                    nc.vector.tensor_tensor(q_rest[:], misc_f, q_parts[:, 0, :], ALU.subtract).then_inc(s["q_rest_ready"], 1)
                elif name == "k":
                    dve.wait_ge(s["k_high"], b + 1)
                    if not (isinstance(b, int) and b == 0):
                        dve.wait_ge(s["k_split"], b)
                    nc.vector.tensor_tensor(k_rest[:], misc_f, k_parts[:, 0, :], ALU.subtract).then_inc(s["k_rest_ready"], 1)
                elif name in ("o0", "o1", "o2", "o3"):
                    k = int(name[1])
                    dve.wait_ge(s["misc_full"], use + 1)
                    o = misc_f.rearrange("p (h w) -> p h w", w=VW)
                    nc.vector.reciprocal(sums_inv[:, k, :], o[:, :, DH]).then_inc(s["sums_ready"], 1)
                    dve.wait_ge(s["sums_ready"], CH * b + k + 1)
                    nc.vector.tensor_tensor(attn[:, k, :].rearrange("p (h d) -> p h d", h=H), o[:, :, 0:DH],
                                            sums_inv[:, k, :].unsqueeze(2).to_broadcast([P, H, DH]), ALU.mult).then_inc(s["attn_ready"], 1)
                elif name == "proj":
                    dve.wait_ge(s["misc_full"], use + 1)
                    row = x_all[:, bass.ds(b, 1), :, :].rearrange("p o k c -> p (o k c)")
                    nc.vector.tensor_tensor(row, misc_f, row, ALU.add).then_inc(s["x1_ready"], 1)
                elif name == "router":
                    logits = misc_f[:, 0:CH * E].rearrange("p (k e) -> p k e", e=E)
                    dve.wait_ge(s["misc_full"], use + 1)
                    nc.vector.tensor_reduce(r_max[:], logits, AX.X, ALU.max).then_inc(s["r_max_ready"], 1)
                    dve.wait_ge(s["r_max_ready"], b + 1)
                    nc.vector.tensor_tensor(r_logit[:], logits, r_max[:].unsqueeze(2).to_broadcast([P, CH, E]),
                                            ALU.subtract).then_inc(s["r_logit_ready"], 1)

            def ln2_stats(b, k):
                if k == 0:
                    dve.wait_ge(s["x1_ready"], b + 1)
                    dve.sem_inc(s["waited"])
                if k < CH - 1:
                    bn_stats(b, bn2, k)
                elif k < CH:
                    bn_stats(b, bn2, k).then_inc(s["ln2_bn"], 1)
                else:
                    bn_aggregate(b, bn2, mv2, "ln2_bn").then_inc(s["ln2_mv"], 1)

            def softmax_sum(b):
                dve.wait_ge(s["r_exp_ready"], b + 1)
                nc.vector.tensor_reduce(r_sum[:], r_exp[:], AX.X, ALU.add).then_inc(s["r_sum_ready"], 1)
                dve.wait_ge(s["r_sum_ready"], b + 1)
                nc.vector.reciprocal(r_inv[:], r_sum[:]).then_inc(s["r_inv_ready"], 1)

            def sort(b):
                dve.wait_ge(s["r_score_ready"], b + 1)
                dve.sem_inc(s["waited"])
                for k in range(CH):
                    last = nc.vector.max(r_sorted[:, k, :], r_score[:, k, 0:E])
                last.then_inc(s["r_sorted_ready"], 1)

            def pick(b):
                dve.wait_ge(s["r_sorted_ready"], b + 1)
                nc.vector.tensor_copy(r_top[:, :, 0:2], r_sorted[:, :, 0:2]).then_inc(s["r_top_ready"], 1)
                dve.wait_ge(s["r_top_ready"], b + 1)
                dve.sem_inc(s["waited"])
                for k in range(CH):
                    last = nc.vector.match_replace(r_without[:, k, :], r_top[:, k, :], r_score[:, k, :], 0.0)
                last.then_inc(s["r_without_ready"], 1)

            def denominator(b):
                dve.wait_ge(s["r_den_ready"], 2 * (b + 1))
                nc.vector.reciprocal(r_den_inv[:], r_den_eps[:]).then_inc(s["r_den_inv_ready"], 1)

            dve.wait_ge(s["x0_loaded"], 16)
            ln1_stats(0)
            dve.wait_ge(s["mod_full"], 1)
            nc.vector.tensor_copy(cT[:], s_col[0][:, 0, 0:B]).then_inc(s["cT_ready"], 1)
            dve.wait_ge(s["wqkv_loaded"], 16)
            for i in range(2):
                last = nc.vector.tensor_copy(wqk_sb[:, i, :].rearrange("c (a d r) -> c a d r", a=2, d=DH),
                                             wqkv_sb[:, C * i:C * (i + 1)].rearrange("c (r a d) -> c a d r", a=2, d=DH))
            last.then_inc(s["wqk_ready"], 1)
            dve.wait_ge(s["mod_full"], 2)
            nc.vector.tensor_copy(mod[:].rearrange("p j b -> p (j b)"), s_col[0][:, 1, 0:NJ * B]).then_inc(s["mod_step"], 1)
            dve.wait_ge(s["mod_step"], 1)
            nc.vector.tensor_scalar(mod[:, CA, :], mod[:, CA, :], 1.0, None, ALU.add)
            nc.vector.tensor_scalar(mod[:, CB, :], mod[:, CB, :], 1.0, None, ALU.add).then_inc(s["mod_ready"], 1)
            g, twice, size = mod[:, GA::GB - GA, :], mod_tmp[:, 0], mod_tmp[:, 1]
            nc.vector.tensor_scalar(twice, g, 0.0, 2.0, ALU.is_ge, ALU.mult).then_inc(s["mod_step"], 1)
            dve.wait_ge(s["mod_step"], 2)
            nc.vector.scalar_tensor_tensor(out=size, in0=twice, scalar=-1.0, in1=g, op0=ALU.add, op1=ALU.mult).then_inc(s["mod_step"], 1)
            dve.wait_ge(s["mod_step"], 3)
            nc.vector.tensor_scalar(size, size, GATE_MIN, None, ALU.max).then_inc(s["mod_step"], 1)
            dve.wait_ge(s["mod_step"], 4)
            nc.vector.scalar_tensor_tensor(out=g, in0=twice, scalar=-1.0, in1=size, op0=ALU.add, op1=ALU.mult).then_inc(s["mod_ready"], 1)

            dve.wait_ge(s["x_loaded"], 16)
            for name in PROJECT:
                evacuate(misc_use(0, None, None, name), 0, 0, name)
                for b in {"q": range(1, 4), "k": range(4, B)}.get(name, ()):
                    ln1_stats(b)
            dve.wait_ge(s["mod_full"], 3)
            nc.vector.tensor_copy(ga_rows[:].rearrange("p b c -> p (b c)"), s_col[1][:].rearrange("p i n -> p (i n)")).then_inc(s["mod_ready"], 1)
            for t in range(AHEAD):
                for j in range(G):
                    row_max(0, 0, t, j)

            REST = {(2, 1): "q", (3, 1): "k"}
            LN2_STATS = [(7, 1), (8, 0), (8, 1), (9, 0), (9, 1)]
            ROUTE = {(12, 1): softmax_sum, (13, 0): sort, (13, 1): pick, (14, 0): denominator}

            def body(b, par, first, last):
                for t in range(SLOTS):
                    for half in range(2):
                        if t < SLOTS - AHEAD:
                            for j in range(2 * half, 2 * half + 2):
                                row_max(b, par, t + AHEAD, j)
                        elif not last:
                            for j in range(2 * half, 2 * half + 2):
                                row_max(b + 1, 1 - par, t + AHEAD - SLOTS, j)
                        at = (t, half)
                        if not first:
                            if at in LN2_STATS:
                                ln2_stats(b - 1, LN2_STATS.index(at))
                            if at in ROUTE:
                                ROUTE[at](b - 1)
                        if at in REST and not last:
                            evacuate(None, b + 1, 1 - par, REST[at])
                        name = TASKS.get(at)
                        if name in tasks(first, last) and name not in REST.values():
                            of = owner(b, name)
                            evacuate(misc_use(b, first, last, name), of, 1 - par if of is not b else par, name)

            dve.wait_ge(s["top_const"], 1)
            over_batches(dve, body)

            def finish(b):
                dve.wait_ge(s["y_back"], b + 1)
                if not (isinstance(b, int) and b == 0):
                    dve.wait_ge(s["result_stored"], 16 * b)
                nc.vector.tensor_tensor(result, misc_f, x_all[:, bass.ds(b, 1), :, :].rearrange("p o k c -> p (o k c)"),
                                        ALU.add).then_inc(s["result_ready"], 1)

            def block_body(b, par, first, last):
                for k in range(KT):
                    i = KT * b + k
                    at = (par + k) % 2
                    dve.wait_ge(s["gate_acted"], i + 1)
                    dve.wait_ge(s["up_ready"], i + 1)
                    nc.vector.tensor_tensor(gated[at], gate_act[at], u_ps[at], ALU.mult).then_inc(s["gated_ready"], 1)
                    dve.wait_ge(s["gated_ready"], i + 1)
                    dve.wait_ge(s["comb_ready"], i + 1)
                    if not (first and k < 2):
                        dve.wait_ge(s["hid_split"], i - 1)
                    nc.vector.tensor_tensor(weighed[at], gated[at], c_ps[at], ALU.mult).then_inc(s["weighed_ready"], 1)
                    if k == BACK + 1 and not first:
                        finish(b - 1)
                    if first:
                        for name in TAIL_AT.get(k, ()):
                            evacuate(tail_use(TAIL.index(name)), B - 1, 1, name)
                        if k == 3:
                            for step in range(CH + 1):
                                ln2_stats(B - 1, step)
                        elif k == 7:
                            softmax_sum(B - 1)
                        elif k == 8:
                            sort(B - 1)
                            pick(B - 1)
                        elif k == 9:
                            denominator(B - 1)

            over_batches(dve, block_body)
            finish(B - 1)

        @block.tensor
        def _(pe):
            def free(b, name):
                if name == "xT":
                    pe.wait_ge(s["hT_ready"], b + 1)
                elif name == "q":
                    pe.wait_ge(s["q_rest_ready"], b + 1)
                elif name == "k":
                    pe.wait_ge(s["k_rest_ready"], b + 1)
                elif name == "v":
                    pe.wait_ge(s["v_ready"], b + 1)
                elif name.startswith("max"):
                    pe.wait_ge(s["maxT_ready"], group(b, int(name[3:])) + 1)
                elif name in ("o0", "o1", "o2", "o3"):
                    pe.wait_ge(s["attn_ready"], CH * b + int(name[1]) + 1)
                elif name == "attnT":
                    pe.wait_ge(s["attnT_ready"], b + 1)
                elif name == "proj":
                    pe.wait_ge(s["x1_ready"], b + 1)
                elif name == "x1T":
                    pe.wait_ge(s["h2T_ready"], b + 1)
                elif name == "router":
                    pe.wait_ge(s["r_logit_ready"], b + 1)
                elif name == "combT":
                    pe.wait_ge(s["combT_ready"], b + 2)

            def task(b, par, name):
                if name == "xT":
                    pe.wait_ge(s["xn_ready"], b + 1)
                    for k in range(CH):
                        last = nc.tensor.transpose(misc_f[:, P * k:P * (k + 1)], xn[:, k, :], ident[:])
                elif name == "q":
                    last = nc.tensor.matmul(misc_f, wqk_sb[:, 0, :], hT[:], start=True, stop=True)
                elif name == "k":
                    last = nc.tensor.matmul(misc_f, wqk_sb[:, 1, :], hT[:], start=True, stop=True)
                elif name == "v":
                    for k in range(CH):
                        last = nc.tensor.matmul(misc_f[:, C * k:C * (k + 1)], hT[:, P * k:P * (k + 1)], wqkv_sb[:, 2 * C:3 * C],
                                                start=True, stop=True)
                elif name.startswith("max"):
                    pe.wait_ge(s["max_split"], 4 * (group(b, int(name[3:])) + 1))
                    pe.sem_inc(s["waited"])
                    last = nc.tensor.transpose(misc_16[0:G * 3 * CH, 0:P], negmax_parts[:].rearrange("p g s k -> p (g s k)"), ident16[:])
                elif name in ("o0", "o1", "o2", "o3"):
                    k = int(name[1])
                    if k == 0:
                        pe.wait_ge(s["o_saved"], NG * (b + 1))
                    for n in range(NG):
                        last = nc.tensor.transpose(misc_f[:, P * n:P * (n + 1)], oT[par][:, n, P * k:P * (k + 1)], ident[:])
                elif name == "attnT":
                    for k in range(CH):
                        last = nc.tensor.transpose(misc_f[:, P * k:P * (k + 1)], attn[:, k, :], ident[:])
                elif name == "proj":
                    pe.wait_ge(s["attnT_ready"], b + 1)
                    pe.wait_ge(s["wo_ga_ready"], b + 1)
                    for k in range(CH):
                        last = nc.tensor.matmul(misc_f[:, C * k:C * (k + 1)], attnT[:, P * k:P * (k + 1)], wo_ga[:], start=True, stop=True)
                elif name == "x1T":
                    pe.wait_ge(s["x1n_ready"], b + 1)
                    for k in range(CH):
                        last = nc.tensor.transpose(misc_f[:, P * k:P * (k + 1)], x1n[:, k, :], ident[:])
                elif name == "router":
                    pe.wait_ge(s["wr_loaded"], 16)
                    for k in range(CH):
                        last = nc.tensor.matmul(misc_f[:, E * k:E * (k + 1)], h2T[:, P * k:P * (k + 1)], wr_sb[:], start=True, stop=True)
                elif name == "combT":
                    pe.wait_ge(s["comb_split"], 4 * (b + 1))
                    for k in range(CH):
                        last = nc.tensor.transpose(misc_16[0:3 * E, P * k:P * (k + 1)], comb_parts[:, k, :, :].rearrange("p s e -> p (s e)"), ident16[:])
                last.then_inc(s["misc_full"], 1)

            def row_scores(b, par, t, j):
                n, qc = t // CH, t % CH
                head = G * n + j
                unit = G * (SLOTS * b + t) + j
                at = 64 * (head % 2)
                if t == 0 and j == 0:
                    pe.wait_ge(s["stacked"], 16 * LOADS * (b + 1))
                if not (isinstance(b, int) and b == 0 and t == 0 and j < 2):
                    pe.wait_ge(s["row_max"], unit - 1)
                nc.tensor.matmul(s_row[j % 2][:, 0, :], q_stack[par][at:at + KS, head // 2, P * qc:P * (qc + 1)],
                                 k_stack[par][at:at + KS, head // 2, :], start=True, stop=True).then_inc(s["row_ready"], 1)

            def col_scores(b, par, t, pp):
                n, kc = t // CH, t % CH
                unit = 2 * (SLOTS * b + t) + pp
                pair = 2 * n + pp
                if kc == 0 and pp == 0:
                    pe.wait_ge(s["max_loaded"], 32 * (group(b, n) + 1))
                if not (isinstance(b, int) and b == 0 and t == 0):
                    pe.wait_ge(s["exp_done"], unit - 1)
                for a in range(2):
                    last = nc.tensor.matmul(s_col[pp][:, a, :], k_stack[par][64 * a:64 * a + KS, pair, P * kc:P * (kc + 1)],
                                            q_stack[par][64 * a:64 * a + KS, pair, :], start=True, stop=True)
                last.then_inc(s["col_ready"], 1)

            def weigh(b, par, t):
                n, kc = t // CH, t % CH
                pe.wait_ge(s["exp_done"], 2 * (SLOTS * b + t) + 2)
                if kc == 0 and not (isinstance(b, int) and b == 0 and n == 0):
                    pe.wait_ge(s["o_saved"], group(b, n))
                for j in range(G):
                    last = nc.tensor.matmul(o_acc[VW * j:VW * (j + 1), 0, :], v_aug[par][:, kc, G * n + j, :],
                                            probs[t % 2][:, j, :], start=(kc == 0), stop=(kc == CH - 1))
                last.then_inc(s["pv_done"], 1)

            pe.wait_ge(s["c_silu"], 1)
            pe.wait_ge(s["ident_ready"], 1)
            nc.tensor.transpose(s_col[0][:, 0, 0:B], c_act[:], ident[0:B, 0:B]).then_inc(s["mod_full"], 1)
            pe.wait_ge(s["cT_ready"], 1)
            pe.wait_ge(s["wmod_loaded"], 16)
            for j in range(NJ):
                last = nc.tensor.matmul(s_col[0][:, 1, B * j:B * (j + 1)], wmod_sb[:, C * j:C * (j + 1)], cT[:], start=True, stop=True)
            last.then_inc(s["mod_full"], 1)
            for i, name in enumerate(BEFORE):
                if name == "q":
                    pe.wait_ge(s["wqk_ready"], 1)
                if i:
                    free(0, BEFORE[i - 1])
                if name == "max0":
                    pe.wait_ge(s["mod_ready"], 2)
                    for b in range(B):
                        last = nc.tensor.matmul(s_col[1][:, b * C // N, b * C % N:b * C % N + C], mod[:, GA, b:b + 1].to_broadcast([C, P]), ident[:],
                                                start=True, stop=True)
                    last.then_inc(s["mod_full"], 1)
                    pe.wait_ge(s["ident16_ready"], 1)
                    for t in range(CH + 2):
                        for j in range(G):
                            row_scores(0, 0, t, j)
                task(0, 0, name)
            for t in range(CH + 2, AHEAD):
                for j in range(G):
                    row_scores(0, 0, t, j)
            pe.wait_ge(s["mod_ready"], 3)

            def body(b, par, first, last):
                mine = tasks(first, last)
                before = None

                def turn(at):
                    nonlocal before
                    name = TASKS.get(at)
                    if name not in mine:
                        return
                    if before is None:
                        free(b, "max0")
                        if not first:
                            pe.wait_ge(s["combT_ready"], b)
                    else:
                        free(owner(b, before), before)
                    of = owner(b, name)
                    task(of, par if of is b else 1 - par, name)
                    before = name

                for t in range(SLOTS):
                    def scores(j):
                        if t < SLOTS - AHEAD:
                            row_scores(b, par, t + AHEAD, j)
                        elif not last:
                            row_scores(b + 1, 1 - par, t + AHEAD - SLOTS, j)
                    scores(0)
                    scores(1)
                    col_scores(b, par, t, 0)
                    turn((t, 0))
                    scores(2)
                    col_scores(b, par, t, 1)
                    scores(3)
                    turn((t, 1))
                    if t > 0:
                        weigh(b, par, t - 1)
                    elif not first:
                        weigh(b - 1, 1 - par, SLOTS - 1)

            over_batches(pe, body)
            weigh(B - 1, 1, SLOTS - 1)

            pe.wait_ge(s["w_split"], 3)
            pe.wait_ge(s["sel_loaded"], 48)
            pe.wait_ge(s["row_max"], G * SLOTS * B)
            pe.wait_ge(s["exp_done"], 2 * SLOTS * B)
            pe.wait_ge(s["o_saved"], NG * B)

            def product(out_ps, w_hi, w_lo, k, hi, lo, start, stop):
                nc.tensor.matmul(out_ps, w_hi[:, k, :], hi[:], start=start, stop=False)
                nc.tensor.matmul(out_ps, w_hi[:, k, :], lo[:], start=False, stop=False)
                return nc.tensor.matmul(out_ps, w_lo[:, k, :], hi[:], start=False, stop=stop)

            def down(b, k):
                pe.wait_ge(s["hid_split"], KT * b + k + 1)
                if k == 0 and not (isinstance(b, int) and b == 0):
                    pe.wait_ge(s["yT_ready"], b)
                product(y_ps, wd_hi, wd_lo, k, hid_hi[k % HIDDEN], hid_lo[k % HIDDEN],
                        start=(k == 0), stop=(k == KT - 1)).then_inc(s["down_done"], 1)

            def back(b):
                pe.wait_ge(s["yT_ready"], b + 1)
                if isinstance(b, int) and b == 0:
                    free(B - 1, "combT")
                else:
                    pe.wait_ge(s["result_ready"], b)
                for k in range(CH):
                    last = nc.tensor.transpose(misc_f[:, P * k:P * (k + 1)], yT[:, P * k:P * (k + 1)], ident[:])
                last.then_inc(s["y_back"], 1)

            def block_body(b, par, first, last):
                for k in range(KT):
                    i = KT * b + k
                    at = (par + k) % 2
                    if k == 0:
                        pe.wait_ge(s["h_split"], b + 1)
                    if not (first and k < 2):
                        pe.wait_ge(s["gate_acted"], i - 1)
                    product(g_ps[at], wg_hi, wg_lo, k, h_hi[par], h_lo[par], True, True).then_inc(s["gate_ready"], 1)
                    if not (first and k < 2):
                        pe.wait_ge(s["gated_ready"], i - 1)
                    product(u_ps[at], wu_hi, wu_lo, k, h_hi[par], h_lo[par], True, True).then_inc(s["up_ready"], 1)
                    if k == 0:
                        pe.wait_ge(s[f"comb_loaded{par}"], 8 * (b + 2 - par))
                        pe.sem_inc(s["waited"])
                    if not (first and k < 2):
                        pe.wait_ge(s["weighed_ready"], i - 1)
                        pe.sem_inc(s["waited"])
                    nc.tensor.matmul(c_ps[at], sel[:, P * k:P * (k + 1)], comb_rows[:, par, :],
                                     start=True, stop=True).then_inc(s["comb_ready"], 1)
                    if k >= LAG:
                        down(b, k - LAG)
                    elif not first:
                        down(b - 1, KT + k - LAG)
                    if k == BACK and not first:
                        back(b - 1)
                    if first:
                        for name in TAIL_AT.get(k, ()):
                            n = TAIL.index(name)
                            if n:
                                free(B - 1, TAIL[n - 1])
                            else:
                                free(B - 2, "combT")
                            task(B - 1, 1, name)

            over_batches(pe, block_body)
            for k in range(KT - LAG, KT):
                down(B - 1, k)
            back(B - 1)


_INS = ['L0_attn_x', 'L0_attn_w_qkv', 'L0_attn_w_out', 'L0_ffn_w_router', 'L0_ffn_w_gate', 'L0_ffn_w_up', 'L0_ffn_w_down', 'L0_c', 'L0_wmod']


def kernel(**inputs):
    import concourse.bacc as bacc
    import numpy as np
    from concourse.bass_utils import run_bass_kernel_spmd

    nc = bacc.Bacc("TRN2", target_bir_lowering=False, num_devices=1)
    arrays, args = {}, []
    for name in _INS:
        a = np.ascontiguousarray(inputs[name])
        arrays[f"in_{name}"] = a
        args.append(nc.dram_tensor(f"in_{name}", a.shape, mybir.dt.from_np(a.dtype), kind="ExternalInput").ap())
    out = nc.dram_tensor("out", inputs["L0_attn_x"].shape, F32, kind="ExternalOutput").ap()
    adaln_block(nc, *args, out)
    return run_bass_kernel_spmd(nc, [arrays], core_ids=[0]).results[0]["out"]
```

```python
from contextlib import ExitStack

import concourse.bass as bass
from concourse import mybir

F32 = mybir.dt.float32
F32R = mybir.dt.float32r
BF16 = mybir.dt.bfloat16
ALU = mybir.AluOpType
ACT = mybir.ActivationFunctionType
AX = mybir.AxisListType


def adaln_block(nc, x, w_qkv, w_out, w_router, w_gate, w_up, w_down, c, wmod, out):
    B, N, C = x.shape
    E, _, HID = w_gate.shape
    H = 16
    DH = C // H
    P = 128
    CH = N // P
    G = 4
    NG = H // G
    SLOTS = NG * CH
    AHEAD = 8
    NEXT_BLOCK = 4
    BACK = 5
    LAG = 3
    HIDDEN = 4
    PAIRS = H // 2
    SCORES = 3
    NJ = wmod.shape[1] // C
    SA, CA, GA, SB, CB, GB = range(NJ)
    KT = E * HID // P
    KQ = 6 * DH
    KM = KQ + 3
    KS = P // 2
    VW = 32
    INV_SCALE = float(C) ** -0.5
    LN_EPS, TOPK_EPS, GATE_MIN = 1e-5, 1e-20, 0.25
    Q_HIGH, Q_MID, Q_LOW = 0, 1, 2
    K_LOW, K_HIGH, K_MID = 0, 1, 2
    STORES = 2 * 3
    LOADS = 2

    TASKS = {
        (0, 0): "xT", (0, 2): "max1", (1, 0): "q", (2, 0): "k", (3, 0): "o0", (3, 2): "o1", (4, 0): "o2", (4, 2): "max2",
        (5, 0): "o3", (5, 1): "attnT", (6, 0): "proj", (8, 1): "max3", (9, 0): "v", (10, 2): "x1T", (11, 1): "router",
        (12, 1): "max0", (15, 0): "combT",
    }
    PROJECT = ("xT", "q", "k", "v")
    NEXT = PROJECT + ("max0",)
    OUTPUT = ("o0", "o1", "o2", "o3", "attnT", "proj", "x1T", "router", "combT")
    BEFORE = NEXT

    def owner(b, name):
        return b + 1 if name in NEXT else b - 1 if name in OUTPUT else b

    def tasks(first, last):
        names = [TASKS[k] for k in sorted(TASKS)]
        names = [n for n in names if not (first and n in OUTPUT)]
        return [n for n in names if not (last and n in NEXT)]

    def misc_use(b, first, last, name):
        if first is None:
            return BEFORE.index(name)
        base = len(BEFORE)
        if not first:
            base = base + len(tasks(True, False)) + (b - 1) * len(tasks(False, False))
        return base + tasks(first, last).index(name)

    def tail_use(n):
        return len(BEFORE) + len(tasks(True, False)) + (B - 2) * len(tasks(False, False)) \
            + len(tasks(False, True)) + n

    TAIL = OUTPUT
    TAIL_AT = {(0, 1): "o0", (1, 0): "o1", (1, 1): "o2", (2, 0): "o3", (2, 1): "attnT", (3, 0): "proj",
               (6, 1): "x1T", (7, 1): "router", (10, 1): "combT"}

    UNITS = SLOTS * G

    TURN = {"row": G * (1 + AHEAD) + 2, "col": G * 1 + 2}

    def score_bank(kind, u):
        return (u + (SCORES - UNITS % SCORES) * (u >= TURN[kind])) % SCORES

    def score_distance(kind, u):
        return next(d for d in range(1, 2 * SCORES) if score_bank(kind, (u - d) % UNITS) == score_bank(kind, u))

    EXPERT_ROWS = [[(e, max(0, e * HID - P * k), min(P, (e + 1) * HID - P * k))
                    for e in range(E) if e * HID < P * (k + 1) and (e + 1) * HID > P * k] for k in range(KT)]

    def ring_distance(k):
        if k >= HIDDEN:
            return HIDDEN
        return k + KT - max(j for j in range(KT) if j % HIDDEN == k)

    ctx = ExitStack()
    with ctx:
        def sb(name, shape, dt=F32):
            return ctx.enter_context(nc.sbuf_tensor(name, shape, dt))

        def sem(name):
            return ctx.enter_context(nc.semaphore(name))

        def dram(name, shape, dt):
            return nc.dram_tensor(name, shape, dt, kind="Internal").ap()

        q_scr = dram("q_scr", (2, KS, PAIRS, N), BF16)
        k_scr = dram("k_scr", (2, KS, PAIRS, N), BF16)
        max_scr = dram("max_scr", (G * 3 * CH, P), BF16)
        h2T_scr = dram("h2T_scr", (B, C, N), F32)
        combT_scr = dram("combT_scr", (B, E, N), F32)

        wqkv_sb = sb("wqkv_sb", [C, 3 * C])
        wqk_sb = sb("wqk_sb", [C, 2, C])
        wo_sb = sb("wo_sb", [C, C])
        wr_sb = sb("wr_sb", [C, E])
        wmod_sb = sb("wmod_sb", [C, NJ * C])
        c_sb = sb("c_sb", [B, C])
        c_act = sb("c_act", [B, C])
        unused = sb("unused", [B, C])
        cT = sb("cT", [C, B])
        mod = sb("mod", [C, NJ, B])
        mod_tmp = sb("mod_tmp", [C, 2, 2, B])
        ga_rows = sb("ga_rows", [P, B, C])
        ident = sb("ident", [P, P])
        ident16 = sb("ident16", [P, P], BF16)
        neg_half = sb("neg_half", [P, (B - 1) * CH])
        w_raw = sb("w_raw", [P, E * HID])
        wg_hi, wg_lo, wu_hi, wu_lo, wd_hi, wd_lo = (
            sb(n, [P, KT, C], F32R) for n in ("wg_hi", "wg_lo", "wu_hi", "wu_lo", "wd_hi", "wd_lo"))

        bn1 = sb("bn1", [P, B, CH, 6])
        mv1 = sb("mv1", [P, B, CH, 2])
        ve1 = sb("ve1", [P, B, CH])
        negmean1 = sb("negmean1", [P, B, CH])
        shift1 = sb("shift1", [P, B, CH])
        rstd1 = sb("rstd1", [P, B, CH])
        xn = sb("xn", [P, CH, C])
        hT = sb("hT", [C, N])
        q_parts = sb("q_parts", [P, 3, N], BF16)
        k_parts = sb("k_parts", [P, 3, N], BF16)
        q_rest = sb("q_rest", [P, N])
        k_rest = sb("k_rest", [P, N])
        q_stack = [sb(f"q_stack{i}", [P, PAIRS, N], BF16) for i in range(2)]
        k_stack = [sb(f"k_stack{i}", [P, PAIRS, N], BF16) for i in range(2)]
        v_aug = [sb(f"v_aug{i}", [P, CH, H, VW]) for i in range(2)]

        negmax = [sb(f"negmax{i}", [P, G, CH]) for i in range(2)]
        negmax_rest = sb("negmax_rest", [P, G, CH])
        negmax_parts = sb("negmax_parts", [P, G, 3, CH], BF16)
        more_rows = sb("more_rows", [KS - KQ, 2, C], BF16)
        negmax_T = sb("negmax_T", [G * 3 * CH, P], BF16)
        probs = [sb(f"probs{i}", [P, G, N]) for i in range(2)]
        oT = [sb(f"oT{i}", [P, NG, N]) for i in range(2)]

        sums_inv = sb("sums_inv", [P, CH, H])
        attn = sb("attn", [P, CH, C])
        attnT = sb("attnT", [C, N])
        wo_ga = sb("wo_ga", [C, C])
        bn2 = sb("bn2", [P, CH, 6])
        mv2 = sb("mv2", [P, CH, 2])
        ve2 = sb("ve2", [P, CH])
        negmean2 = sb("negmean2", [P, CH])
        shift2 = sb("shift2", [P, CH])
        rstd2 = sb("rstd2", [P, CH])
        x1n = sb("x1n", [P, CH, C])
        h2T = sb("h2T", [C, N])
        r_max = sb("r_max", [P, CH])
        r_logit = sb("r_logit", [P, CH, E])
        r_exp = sb("r_exp", [P, CH, E])
        r_sum = sb("r_sum", [P, CH])
        r_inv = sb("r_inv", [P, CH])
        r_score = sb("r_score", [P, CH, 2 * E])
        r_sorted = sb("r_sorted", [P, CH, E])
        r_top = sb("r_top", [P, CH, E])
        r_without = sb("r_without", [P, CH, 2 * E])
        r_den = sb("r_den", [P, CH])
        r_den_eps = sb("r_den_eps", [P, CH])
        r_den_inv = sb("r_den_inv", [P, CH])
        r_picked = sb("r_picked", [P, CH, E])
        comb = sb("comb", [P, CH, E])
        combT = sb("combT", [E, N])

        x_all = sb("x_all", [P, B, CH, C])

        gate_act = [probs[0][:, i, :] for i in range(2)]
        weighed = [probs[1][:, i, :] for i in range(2)]
        yT = probs[0][:, 2, :]
        h_raw = oT[0][:, 0, :]
        result = probs[1][:, 2, :]
        gated = [probs[i][:, 3, :] for i in range(2)]
        spread = [stack_sb[:, 2 * i:2 * i + 2, :].rearrange("p i n -> p (i n)").bitcast(F32)
                  for stack_sb in (q_stack[0], k_stack[0], q_stack[1]) for i in range(PAIRS // 2)][0:KT]
        h_hi, h_lo = ([sb(f"{n}{i}", [C, N], F32R) for i in range(2)] for n in ("h_hi", "h_lo"))
        hid_hi, hid_lo = ([sb(f"{n}{i}", [P, N], F32R) for i in range(HIDDEN)] for n in ("hid_hi", "hid_lo"))

        def bank(name):
            return ctx.enter_context(nc.psum_tensor(name, [P, N], F32))

        s_row = [bank(f"s_row{i}") for i in range(SCORES)]
        s_col = [bank(f"s_col{i}") for i in range(SCORES)]
        o_acc = bank("o_acc")
        misc = bank("misc")
        misc_f = misc[:]
        misc_16 = misc[:].bitcast(BF16)

        def k_bank(b):
            return s_row[SCORES - 1][:] if isinstance(b, int) and b == 0 else misc_f

        g_ps, u_ps = ([a[:], b[:]] for a, b in (s_row[0:2], s_col[0:2]))
        y_ps = o_acc[:]
        ga_banks = [s_col[0], s_col[2]]

        names = """
            c_loaded wqkv_loaded wo_loaded wr_loaded wmod_loaded w_loaded x0_loaded x_loaded
            ident_zeroed ident_ready ident16_ready half_ready
            v_zeroed v_const more_ready more_stored top_const wqk_ready
            c_silu cT_ready mod_full mod_step mod_ready w_high w_split
            ln1_bn ln1_mv ln1_step ln1_ready ln1_scaled xn_ready
            hT_ready q_high k_high q_rest_ready k_rest_ready q_mid k_mid q_split k_split v_ready
            q_stored k_stored stacked_first stacked
            misc_full row_ready row_max max_split maxT_ready max_stored max_loaded
            col_ready exp_done pv_done o_saved
            sums_ready attn_ready attnT_ready wo_ga_ready x1_ready
            ln2_bn ln2_mv ln2_step ln2_ready ln2_scaled x1n_ready h2T_ready h2T_kept
            r_max_ready r_logit_ready r_exp_ready r_sum_ready r_inv_ready r_score_ready r_sorted_ready
            r_top_ready r_without_ready r_den_ready r_den_inv_ready comb_step combT_ready combT_kept
            h_loaded h_high h_split gate_ready up_ready gate_acted gated_ready weighed_ready
            hid_high hid_split down_done yT_ready y_back result_ready result_stored waited
        """.split()
        names += [f"spread{k}_loaded" for k in range(KT)]
        s = {n: sem(n) for n in names}


        block = ctx.enter_context(nc.Block())

        def over_batches(eng, body):
            body(0, 0, True, False)
            with eng.Fori(0, (B - 2) // 2) as i:
                body(2 * i + 1, 1, False, False)
                body(2 * i + 2, 0, False, False)
            body(B - 1, 1, False, True)

        def group(b, n):
            return NG * b + n

        @block.sync
        def _(sp):
            by_rows = "b (k p) c -> p b k c"
            sp.dma_start(x_all[:, 0:1, :, :], x[0:1].rearrange(by_rows, p=P)).then_inc(s["x0_loaded"], 16)
            sp.dma_start(c_sb[:], c).then_inc(s["c_loaded"], 16)
            sp.dma_start(wmod_sb[:], wmod).then_inc(s["wmod_loaded"], 16)
            sp.dma_start(wqkv_sb[:], w_qkv).then_inc(s["wqkv_loaded"], 16)
            sp.dma_start(x_all[:, 1:B, :, :], x[1:B].rearrange(by_rows, p=P)).then_inc(s["x_loaded"], 16)
            sp.dma_start(wo_sb[:], w_out).then_inc(s["wo_loaded"], 16)
            sp.dma_start(wr_sb[:], w_router).then_inc(s["wr_loaded"], 16)

            def store_parts(b, scr, pairs, mid, split, stored):
                sp.wait_ge(s[mid], b + 1)
                for i, pair in enumerate(pairs):
                    if i == 2:
                        sp.wait_ge(s[split], b + 1)
                    for a in range(2):
                        to = scr[a, 2 * DH * i:2 * DH * (i + 1)].rearrange("(t d) r n -> (d r) t n", d=DH)
                        sp.dma_start(to, pair[64 * a:64 * (a + 1)]).then_inc(s[stored], 16)

            def load_stacks(b, par):
                if isinstance(b, int) and b == 0:
                    sp.wait_ge(s["more_stored"], 16 * 4)
                sp.wait_ge(s["q_stored"], 16 * STORES * (b + 1))
                sp.wait_ge(s["k_stored"], 16 * STORES * (b + 1))
                for r0, r1, stacked in ((0, G // 2, "stacked_first"), (G // 2, PAIRS, "stacked")):
                    for stack_sb, scr in ((q_stack[par], q_scr), (k_stack[par], k_scr)):
                        sp.dma_start(stack_sb[:, r0:r1, :], scr.rearrange("a m r n -> (a m) r n")[:, r0:r1]).then_inc(s[stacked], 16)

            def stack(b, par):
                if not (isinstance(b, int) and b == 0):
                    sp.wait_ge(s["stacked"], 16 * LOADS * b)
                    sp.sem_inc(s["waited"])
                twice = [P, 2, N]
                store_parts(b, q_scr, (q_parts[:, Q_HIGH:Q_MID + 1], q_parts[:, Q_HIGH:Q_MID + 1], q_parts[:, Q_HIGH:Q_LOW + 1:Q_LOW - Q_HIGH]),
                            "q_mid", "q_split", "q_stored")
                store_parts(b, k_scr, (k_parts[:, K_HIGH:K_HIGH + 1].to_broadcast(twice), k_parts[:, K_MID:K_MID + 1].to_broadcast(twice),
                                       k_parts[:, K_LOW:K_HIGH + 1]), "k_mid", "k_split", "k_stored")
                load_stacks(b, par)

            def keep_h2T(b):
                sp.wait_ge(s["h2T_ready"], b + 1)
                sp.sem_inc(s["waited"])
                sp.dma_start(h2T_scr[bass.ds(b, 1)].rearrange("o c n -> c (o n)"), h2T[:]).then_inc(s["h2T_kept"], 16)

            def keep_combT(b):
                sp.wait_ge(s["combT_ready"], b + 2)
                sp.sem_inc(s["waited"])
                sp.dma_start(combT_scr[bass.ds(b, 1)].rearrange("o e n -> e (o n)"), combT[:]).then_inc(s["combT_kept"], 16)

            sp.wait_ge(s["more_ready"], 2)
            for i, scr in enumerate((q_scr, k_scr)):
                for a in range(2):
                    sp.dma_start(scr[a, KQ:KS].rearrange("m r (i c) -> m (r i) c", c=C),
                                 more_rows[:, i, :].unsqueeze(1).to_broadcast([KS - KQ, PAIRS * N // C, C])).then_inc(s["more_stored"], 16)

            def fetch_h(b):
                if isinstance(b, int) and b == 0:
                    sp.wait_ge(s["attn_ready"], CH * (B - 1))
                else:
                    sp.wait_ge(s["h_split"], b)
                sp.wait_ge(s["h2T_kept"], 16 * (b + 1))
                sp.sem_inc(s["waited"])
                sp.dma_start(h_raw, h2T_scr[bass.ds(b, 1)].rearrange("o c n -> c (o n)")).then_inc(s["h_loaded"], 16)

            def spread_weights(b, k):
                if isinstance(b, int) and b == 0:
                    if k in (0, PAIRS):
                        sp.wait_ge(s["exp_done"], UNITS * (B - 1 if k == 0 else B))
                    if k == 0:
                        sp.wait_ge(s["combT_kept"], 16)
                else:
                    if k == 0:
                        sp.wait_ge(s["combT_kept"], 16 * (b + 1))
                    sp.wait_ge(s["weighed_ready"], KT * (b - 1) + k + 1)
                    sp.sem_inc(s["waited"])
                for e, r0, r1 in EXPERT_ROWS[k]:
                    sp.dma_start(spread[k][r0:r1], combT_scr[bass.ds(b, 1), e, :].to_broadcast([r1 - r0, N])).then_inc(s[f"spread{k}_loaded"], 16)

            stack(0, 0)

            def load_weights(i):
                if i:
                    sp.wait_ge(s["w_split"], i)
                if i < 2:
                    sp.dma_start(w_raw[:].rearrange("d (e h) -> d e h", e=E), (w_gate, w_up)[i].rearrange("e d h -> d e h")).then_inc(s["w_loaded"], 16)
                else:
                    sp.dma_start(w_raw[:].rearrange("p (k d) -> p k d", k=KT),
                                 w_down.rearrange("e h d -> (e h) d").rearrange("(k p) d -> p k d", p=P)).then_inc(s["w_loaded"], 16)

            def body(b, par, first, last):
                if not last:
                    stack(b + 1, 1 - par)
                if first:
                    load_weights(0)
                if last:
                    load_weights(1)
                    load_weights(2)
                if not first:
                    keep_h2T(b - 1)
                if last:
                    fetch_h(0)
                    for k in range(PAIRS):
                        spread_weights(0, k)
                if not first:
                    keep_combT(b - 1)

            over_batches(sp, body)

            def store_result(b):
                sp.wait_ge(s["result_ready"], b + 1)
                sp.sem_inc(s["waited"])
                sp.dma_start(out[bass.ds(b, 1)].rearrange("o (k p) c -> p (o k) c", p=P),
                             result.rearrange("p (k c) -> p k c", c=C)).then_inc(s["result_stored"], 16)

            def block_body(b, par, first, last):
                for k in range(KT):
                    if k == 0 and not last:
                        fetch_h(b + 1)
                    if k == BACK + 2 and not first:
                        store_result(b - 1)
                    if k == BACK + 2 and first:
                        keep_h2T(B - 1)
                    if not last:
                        spread_weights(b + 1, k)
                if first:
                    keep_combT(B - 1)

            for k in range(PAIRS, KT):
                spread_weights(0, k)
            over_batches(sp, block_body)
            store_result(B - 1)
            sp.wait_ge(s["result_stored"], 16 * B)

        @block.gpsimd
        def _(pool):
            nc.gpsimd.memset(ident[:], 0.0).then_inc(s["ident_zeroed"], 1)
            pool.wait_ge(s["ident_zeroed"], 1)
            nc.gpsimd.affine_select(out=ident[:], in_=ident[:], compare_op=ALU.not_equal, fill=1.0, base=0,
                                    pattern=[[-1, P]], channel_multiplier=1).then_inc(s["ident_ready"], 1)
            nc.gpsimd.memset(more_rows[:, 0, :], 0.0).then_inc(s["more_ready"], 1)
            nc.gpsimd.memset(more_rows[:, 1, :], 1.0).then_inc(s["more_ready"], 1)
            nc.gpsimd.memset(neg_half[:], -0.5).then_inc(s["half_ready"], 1)

            def constants(par):
                nc.gpsimd.memset(v_aug[par][:], 0.0).then_inc(s["v_zeroed"], 1)
                pool.wait_ge(s["v_zeroed"], par + 1)
                nc.gpsimd.memset(v_aug[par][:, :, :, DH], 1.0).then_inc(s["v_const"], 1)

            def ln_factors(n, mv, ve, negmean, rstd, shift, ln):
                pool.wait_ge(s[f"{ln}_mv"], n + 1)
                pool.sem_inc(s["waited"])
                nc.gpsimd.tensor_scalar(ve, mv[:, :, 1], LN_EPS, None, ALU.add)
                nc.gpsimd.tensor_scalar(negmean, mv[:, :, 0], -1.0, None, ALU.mult).then_inc(s[f"{ln}_step"], 1)
                pool.wait_ge(s[f"{ln}_step"], 2 * n + 1)
                nc.gpsimd.tensor_tensor(rstd, ve, neg_half[:, 0:rstd.shape[1]], ALU.pow).then_inc(s[f"{ln}_step"], 1)
                pool.wait_ge(s[f"{ln}_step"], 2 * n + 2)
                nc.gpsimd.tensor_tensor(shift, negmean, rstd, ALU.mult).then_inc(s[f"{ln}_ready"], 1)

            def normalise(b, out_sb, rstd, shift, ln, ready):
                whole = [P, CH, C]
                nc.gpsimd.tensor_tensor(out_sb[:], x_all[:, bass.ds(b, 1), :, :].rearrange("p o k c -> p (o k) c"),
                                        rstd.unsqueeze(2).to_broadcast(whole), ALU.mult).then_inc(s[f"{ln}_scaled"], 1)
                pool.wait_ge(s[f"{ln}_scaled"], b + 1)
                nc.gpsimd.tensor_tensor(out_sb[:], out_sb[:], shift.unsqueeze(2).to_broadcast(whole), ALU.add).then_inc(s[ready], 1)

            def normalise1(b):
                if isinstance(b, int) and b < 2:
                    pool.wait_ge(s["ln1_ready"], b + 1)
                if not (isinstance(b, int) and b == 0):
                    pool.wait_ge(s["hT_ready"], b)
                flat = "p o k -> p (o k)"
                normalise(b, xn, rstd1[:, bass.ds(b, 1), :].rearrange(flat), shift1[:, bass.ds(b, 1), :].rearrange(flat), "ln1", "xn_ready")

            def normalise2(b):
                pool.wait_ge(s["ln2_ready"], b + 1)
                normalise(b, x1n, rstd2[:], shift2[:], "ln2", "x1n_ready")

            def ln1_factors(n, b0, b1):
                flat = "p b k -> p (b k)"
                ln_factors(n, mv1[:, b0:b1].rearrange("p b k m -> p (b k) m"), ve1[:, b0:b1].rearrange(flat), negmean1[:, b0:b1].rearrange(flat),
                           rstd1[:, b0:b1].rearrange(flat), shift1[:, b0:b1].rearrange(flat), "ln1")

            def low_part(b, low, rest, middle, mid, done):
                pool.wait_ge(s[mid], b + 1)
                nc.gpsimd.tensor_tensor(low, rest[:], middle, ALU.subtract).then_inc(s[done], 1)

            def split_weights(i):
                pool.wait_ge(s["w_high"], i + 1)
                nc.gpsimd.tensor_tensor((wg_lo, wu_lo, wd_lo)[i][:].rearrange("p k c -> p (k c)"), w_raw[:],
                                        (wg_hi, wu_hi, wd_hi)[i][:].rearrange("p k c -> p (k c)"), ALU.subtract).then_inc(s["w_split"], 1)

            def split_max(b, n):
                k = group(b, n)
                m = negmax[n % 2]
                pool.wait_ge(s["row_max"], G * CH * (k + 1))
                if not (isinstance(b, int) and b == 0 and n == 0):
                    pool.wait_ge(s["maxT_ready"], k)
                pool.sem_inc(s["waited"])
                nc.gpsimd.tensor_copy(negmax_parts[:, :, 0, :], m[:]).then_inc(s["max_split"], 1)
                pool.wait_ge(s["max_split"], 4 * k + 1)
                nc.gpsimd.tensor_tensor(negmax_rest[:], m[:], negmax_parts[:, :, 0, :], ALU.subtract).then_inc(s["max_split"], 1)
                pool.wait_ge(s["max_split"], 4 * k + 2)
                pool.sem_inc(s["waited"])
                nc.gpsimd.tensor_copy(negmax_parts[:, :, 1, :], negmax_rest[:]).then_inc(s["max_split"], 1)
                pool.wait_ge(s["max_split"], 4 * k + 3)
                nc.gpsimd.tensor_tensor(negmax_parts[:, :, 2, :], negmax_rest[:], negmax_parts[:, :, 1, :], ALU.subtract).then_inc(s["max_split"], 1)

            def fold_ga(b):
                if not (isinstance(b, int) and b == 0):
                    pool.wait_ge(s["x1_ready"], b)
                nc.gpsimd.tensor_tensor(wo_ga[:], wo_sb[:], ga_rows[:, bass.ds(b, 1), :].rearrange("p o c -> p (o c)"), ALU.mult).then_inc(s["wo_ga_ready"], 1)

            def score(b):
                pool.wait_ge(s["r_inv_ready"], b + 1)
                nc.gpsimd.tensor_tensor(r_score[:, :, 0:E], r_exp[:], r_inv[:].unsqueeze(2).to_broadcast([P, CH, E]), ALU.mult).then_inc(s["r_score_ready"], 1)

            def denominator(b):
                pool.wait_ge(s["r_sorted_ready"], b + 1)
                pool.sem_inc(s["waited"])
                nc.gpsimd.tensor_copy(r_top[:, :, 0:2], r_sorted[:, :, 0:2]).then_inc(s["r_top_ready"], 1)
                nc.gpsimd.tensor_tensor(r_den[:], r_sorted[:, :, 0], r_sorted[:, :, 1], ALU.add).then_inc(s["r_den_ready"], 1)
                pool.wait_ge(s["r_den_ready"], 2 * b + 1)
                pool.sem_inc(s["waited"])
                nc.gpsimd.tensor_scalar(r_den_eps[:], r_den[:], TOPK_EPS, None, ALU.add).then_inc(s["r_den_ready"], 1)

            def combine(b):
                pool.wait_ge(s["r_without_ready"], b + 1)
                nc.gpsimd.tensor_tensor(r_picked[:], r_score[:, :, 0:E], r_without[:, :, 0:E], ALU.subtract).then_inc(s["comb_step"], 1)
                pool.wait_ge(s["comb_step"], 2 * b + 1)
                pool.wait_ge(s["r_den_inv_ready"], b + 1)
                pool.wait_ge(s["combT_ready"], b + 1)
                nc.gpsimd.tensor_tensor(comb[:], r_picked[:], r_den_inv[:].unsqueeze(2).to_broadcast([P, CH, E]), ALU.mult).then_inc(s["comb_step"], 1)

            def low_q(b):
                low_part(b, q_parts[:, Q_LOW, :], q_rest, q_parts[:, Q_MID, :], "q_mid", "q_split")

            def low_k(b):
                low_part(b, k_parts[:, K_LOW, :], k_rest, k_parts[:, K_MID, :], "k_mid", "k_split")

            pool.wait_ge(s["half_ready"], 1)
            ln1_factors(0, 0, 1)
            normalise1(0)
            pool.wait_ge(s["ident_ready"], 1)
            nc.gpsimd.tensor_copy(ident16[:], ident[:]).then_inc(s["ident16_ready"], 1)
            constants(0)
            low_q(0)
            low_k(0)
            ln1_factors(1, 1, B)
            constants(1)
            nc.gpsimd.memset(r_score[:, :, E:2 * E], -5.0)
            nc.gpsimd.memset(r_top[:], -5.0).then_inc(s["top_const"], 1)
            split_max(0, 0)
            pool.wait_ge(s["mod_ready"], 3)
            pool.wait_ge(s["wo_loaded"], 16)

            def body(b, par, first, last):
                if not last:
                    normalise1(b + 1)
                split_max(b, 1)
                if last:
                    split_weights(0)
                else:
                    low_q(b + 1)
                if not last:
                    low_k(b + 1)
                split_max(b, 2)
                if not first:
                    fold_ga(b - 1)
                if last:
                    split_weights(1)
                split_max(b, 3)
                if not first:
                    ln_factors(b - 1, mv2[:], ve2[:], negmean2[:], rstd2[:], shift2[:], "ln2")
                    normalise2(b - 1)
                if last:
                    split_weights(2)
                else:
                    split_max(b + 1, 0)
                if not first:
                    score(b - 1)
                    denominator(b - 1)
                    combine(b - 1)

            over_batches(pool, body)

            def hid_low(b, par, k):
                pool.wait_ge(s["hid_high"], KT * b + k + 1)
                nc.gpsimd.tensor_tensor(hid_lo[k % HIDDEN][:], weighed[(par + k) % 2], hid_hi[k % HIDDEN][:], ALU.subtract).then_inc(s["hid_split"], 1)

            def block_low(b, par):
                pool.wait_ge(s["h_high"], b + 1)
                pool.sem_inc(s["waited"])
                nc.gpsimd.tensor_tensor(h_lo[par][:], h_raw, h_hi[par][:],
                                        ALU.subtract).then_inc(s["h_split"], 1)

            def block_body(b, par, first, last):
                for k in range(KT - 1 if last else KT):
                    if first:
                        if k == 0:
                            fold_ga(B - 1)
                        elif k == 3:
                            ln_factors(B - 1, mv2[:], ve2[:], negmean2[:], rstd2[:], shift2[:], "ln2")
                        elif k == 7:
                            score(B - 1)
                        elif k == 8:
                            denominator(B - 1)
                            combine(B - 1)
                    if k == NEXT_BLOCK and not last:
                        block_low(b + 1, 1 - par)
                    hid_low(b, par, k)

            block_low(0, 0)
            over_batches(pool, block_body)

        @block.scalar
        def _(act):
            act.wait_ge(s["c_loaded"], 16)
            nc.scalar.activation(c_act[:], c_sb[:], ACT.Silu).then_inc(s["c_silu"], 1)

            def load_table(function):
                nc.scalar.activation(unused[:], c_sb[:], function, scale=0.0)

            def exp(b, t, j):
                u = G * t + j
                act.wait_ge(s["col_ready"], UNITS * b + u + 1)
                if j == 0 and not (isinstance(b, int) and b == 0 and t < 2):
                    act.wait_ge(s["pv_done"], SLOTS * b + t - 1)
                nc.scalar.activation(probs[t % 2][:, j, :], s_col[score_bank("col", u)][:], ACT.Exp, scale=INV_SCALE).then_inc(s["exp_done"], 1)

            def save_o(b, par, n):
                act.wait_ge(s["pv_done"], SLOTS * b + CH * (n + 1))
                nc.scalar.activation(oT[par][:, n, :], o_acc[:], ACT.Copy).then_inc(s["o_saved"], 1)

            def middle_part(b, middle, rest, rest_ready, mid):
                act.wait_ge(s[rest_ready], b + 1)
                nc.scalar.activation(middle, rest[:], ACT.Copy).then_inc(s[mid], 1)

            def store_max(b, n):
                act.wait_ge(s["maxT_ready"], group(b, n) + 1)
                nc.scalar.dma_start(max_scr, negmax_T[:]).then_inc(s["max_stored"], 16)

            def place_max(b, par, n):
                act.wait_ge(s["max_stored"], 16 * (group(b, n) + 1))
                rows = max_scr.rearrange("(r a s k) q -> a s r (k q)", r=2, a=2, s=3)
                for a in range(2):
                    nc.scalar.dma_start(q_stack[par][64 * a + KQ:64 * a + KM, 2 * n:2 * n + 2, :], rows[a]).then_inc(s["max_loaded"], 16)

            def evacuate(use, b, par, name):
                if name == "xT":
                    act.wait_ge(s["misc_full"], use + 1)
                    nc.scalar.activation(hT[:], misc_f, ACT.Identity, scale=mod[:, CA, bass.ds(b, 1)],
                                         bias=mod[:, SA, bass.ds(b, 1)]).then_inc(s["hT_ready"], 1)
                elif name == "q":
                    act.wait_ge(s["misc_full"], use + 1)
                    if not (isinstance(b, int) and b == 0):
                        act.wait_ge(s["q_stored"], 16 * STORES * b)
                    nc.scalar.activation(q_parts[:, Q_HIGH, :], misc_f, ACT.Copy).then_inc(s["q_high"], 1)
                elif name == "k":
                    act.wait_ge(s["misc_full"], use + 1)
                    if not (isinstance(b, int) and b == 0):
                        act.wait_ge(s["k_stored"], 16 * STORES * b)
                    nc.scalar.activation(k_parts[:, K_HIGH, :], k_bank(b), ACT.Copy).then_inc(s["k_high"], 1)
                elif name == "v":
                    act.wait_ge(s["misc_full"], use + 1)
                    nc.scalar.activation(v_aug[par][:, :, :, 0:DH], misc_f.rearrange("p (k h d) -> p k h d", k=CH, h=H),
                                         ACT.Copy).then_inc(s["v_ready"], 1)
                elif name.startswith("max"):
                    act.wait_ge(s["misc_full"], use + 1)
                    k = group(b, int(name[3:]))
                    if not (isinstance(b, int) and b == 0 and name == "max0"):
                        act.wait_ge(s["max_loaded"], 32 * k)
                    nc.scalar.activation(negmax_T[:], misc_16[0:G * 3 * CH, 0:P], ACT.Copy).then_inc(s["maxT_ready"], 1)
                elif name == "attnT":
                    act.wait_ge(s["misc_full"], use + 1)
                    nc.scalar.activation(attnT[:], misc_f, ACT.Copy).then_inc(s["attnT_ready"], 1)
                elif name == "x1T":
                    act.wait_ge(s["misc_full"], use + 1)
                    if not (isinstance(b, int) and b == 0):
                        act.wait_ge(s["h2T_kept"], 16 * b)
                    nc.scalar.activation(h2T[:], misc_f, ACT.Identity, scale=mod[:, CB, bass.ds(b, 1)],
                                         bias=mod[:, SB, bass.ds(b, 1)]).then_inc(s["h2T_ready"], 1)
                elif name == "router":
                    act.wait_ge(s["r_logit_ready"], b + 1)
                    nc.scalar.activation(r_exp[:], r_logit[:], ACT.Exp).then_inc(s["r_exp_ready"], 1)
                elif name == "combT":
                    act.wait_ge(s["misc_full"], use + 1)
                    if not (isinstance(b, int) and b == 0):
                        act.wait_ge(s["combT_kept"], 16 * b)
                    nc.scalar.activation(combT[:], misc_f[0:E, :], ACT.Copy).then_inc(s["combT_ready"], 1)

            def split_weights(i):
                act.wait_ge(s["w_loaded"], 16 * (i + 1))
                nc.scalar.activation((wg_hi, wu_hi, wd_hi)[i][:].rearrange("p k c -> p (k c)"), w_raw[:], ACT.Copy).then_inc(s["w_high"], 1)

            def block_high(b, par):
                act.wait_ge(s["h_loaded"], 16 * (b + 1))
                nc.scalar.activation(h_hi[par][:], h_raw, ACT.Copy).then_inc(s["h_high"], 1)

            act.sem_inc(s["combT_ready"])
            act.wait_ge(s["mod_ready"], 1)
            act.wait_ge(s["v_const"], 1)
            for name in BEFORE:
                if name == "max0":
                    load_table(ACT.Exp)
                if name == "v":
                    middle_part(0, q_parts[:, Q_MID, :], q_rest, "q_rest_ready", "q_mid")
                    middle_part(0, k_parts[:, K_MID, :], k_rest, "k_rest_ready", "k_mid")
                evacuate(misc_use(0, None, None, name), 0, 0, name)
                if name.startswith("max"):
                    store_max(0, int(name[3:]))
                    place_max(0, 0, int(name[3:]))

            MIDDLE_Q, MIDDLE_K, ROUTER_EXP, FIRST_BLOCK = (2, 0), (3, 0), (12, 0), (14, 1)
            STORE_MAX = {(1, 0): 1, (5, 0): 2, (9, 0): 3, (13, 0): 0}
            PLACE_MAX = {(2, 0): 1, (6, 0): 2, (10, 0): 3, (14, 0): 0}
            SPLIT_WEIGHTS = {(2, 1): 0, (6, 1): 1, (10, 1): 2}

            def body(b, par, first, last):
                for t in range(SLOTS):
                    for half in range(3):
                        at = (t, half)
                        if at == (0, 0) and first:
                            act.wait_ge(s["v_const"], 2)
                        if half == 0 and t % CH == 1:
                            if t > 1:
                                save_o(b, par, t // CH - 1)
                            elif not first:
                                save_o(b - 1, 1 - par, NG - 1)
                        if at == MIDDLE_Q and not last:
                            middle_part(b + 1, q_parts[:, Q_MID, :], q_rest, "q_rest_ready", "q_mid")
                        if at == MIDDLE_K and not last:
                            middle_part(b + 1, k_parts[:, K_MID, :], k_rest, "k_rest_ready", "k_mid")
                        if at == FIRST_BLOCK and last:
                            block_high(0, 0)
                        for table, step in ((STORE_MAX, store_max), (PLACE_MAX, place_max)):
                            n = table.get(at)
                            if n is None or (n == 0 and last):
                                continue
                            of, of_par = (b + 1, 1 - par) if n == 0 else (b, par)
                            if step is store_max:
                                step(of, n)
                            else:
                                step(of, of_par, n)
                        if half < 2:
                            exp(b, t, 2 * half)
                            exp(b, t, 2 * half + 1)
                        if last and at in SPLIT_WEIGHTS:
                            split_weights(SPLIT_WEIGHTS[at])
                        if at == ROUTER_EXP and not first:
                            evacuate(None, b - 1, 1 - par, "router")
                        name = TASKS.get(at)
                        if name in tasks(first, last) and name != "router":
                            of = owner(b, name)
                            evacuate(misc_use(b, first, last, name), of, 1 - par if of is not b else par, name)

            over_batches(act, body)
            load_table(ACT.Silu)
            save_o(B - 1, 1, NG - 1)

            def hid_high(b, par, k, wait_ring):
                i = KT * b + k
                act.wait_ge(s["weighed_ready"], i + 1)
                if wait_ring:
                    act.wait_ge(s["down_done"], i + 1 - ring_distance(k))
                nc.scalar.activation(hid_hi[k % HIDDEN][:], weighed[(par + k) % 2], ACT.Copy).then_inc(s["hid_high"], 1)

            def scale_y(b):
                act.wait_ge(s["down_done"], KT * (b + 1))
                if not (isinstance(b, int) and b == 0):
                    act.wait_ge(s["y_back"], b)
                nc.scalar.activation(yT, y_ps, ACT.Copy, scale=mod[:, GB, bass.ds(b, 1)]).then_inc(s["yT_ready"], 1)

            def block_body(b, par, first, last):
                for k in range(KT):
                    i = KT * b + k
                    if k == LAG and not first:
                        scale_y(b - 1)
                    if first:
                        name = TAIL_AT.get((k, 0))
                        if name:
                            evacuate(tail_use(TAIL.index(name)), B - 1, 1, name)
                    act.wait_ge(s["gate_ready"], i + 1)
                    if not (first and k < 2):
                        act.wait_ge(s["gated_ready"], i - 1)
                    nc.scalar.activation(gate_act[(par + k) % 2], g_ps[(par + k) % 2], ACT.Silu).then_inc(s["gate_acted"], 1)
                    if k:
                        hid_high(b, par, k - 1, not (first and k - 1 < HIDDEN))
                    elif not first:
                        hid_high(b - 1, 1 - par, KT - 1, True)
                    if k == NEXT_BLOCK and not last:
                        block_high(b + 1, 1 - par)
                    if first:
                        name = TAIL_AT.get((k, 1))
                        if name:
                            evacuate(tail_use(TAIL.index(name)), B - 1, 1, name)

            over_batches(act, block_body)
            hid_high(B - 1, 1, KT - 1, True)
            scale_y(B - 1)

        @block.vector
        def _(dve):
            def bn_stats(b, bn, k):
                return nc.vector.bn_stats(bn[:, k, :], x_all[:, bass.ds(b, 1), k, :].rearrange("p o c -> p (o c)"))

            def bn_aggregate(b, bn, mv, bn_done):
                dve.wait_ge(s[bn_done], b + 1)
                dve.sem_inc(s["waited"])
                for k in range(CH):
                    last = nc.vector.bn_aggr(mv[:, k, :], bn[:, k, :])
                return last

            def ln1_stats(b):
                for k in range(CH):
                    last = bn_stats(b, bn1[:, b], k)
                last.then_inc(s["ln1_bn"], 1)
                last = bn_aggregate(b, bn1[:, b], mv1[:, b], "ln1_bn")
                if b in (0, B - 1):
                    last.then_inc(s["ln1_mv"], 1)

            def row_max(b, par, t, j):
                n, qc = t // CH, t % CH
                u = G * t + j
                dve.wait_ge(s["row_ready"], UNITS * b + u + 1)
                if qc == 0 and j == 0 and not (isinstance(b, int) and b == 0 and n < 2):
                    dve.wait_ge(s["max_split"], 4 * (group(b, n) - 1))
                nc.vector.tensor_reduce(negmax[n % 2][:, j, qc:qc + 1], s_row[score_bank("row", u)][:], AX.X, ALU.max,
                                        negate=True).then_inc(s["row_max"], 1)

            def evacuate(use, b, par, name):
                if name == "q":
                    dve.wait_ge(s["q_high"], b + 1)
                    if not (isinstance(b, int) and b == 0):
                        dve.wait_ge(s["q_split"], b)
                    nc.vector.tensor_tensor(q_rest[:], misc_f, q_parts[:, Q_HIGH, :], ALU.subtract).then_inc(s["q_rest_ready"], 1)
                elif name == "k":
                    dve.wait_ge(s["k_high"], b + 1)
                    if not (isinstance(b, int) and b == 0):
                        dve.wait_ge(s["k_split"], b)
                    nc.vector.tensor_tensor(k_rest[:], k_bank(b), k_parts[:, K_HIGH, :], ALU.subtract).then_inc(s["k_rest_ready"], 1)
                elif name in ("o0", "o1", "o2", "o3"):
                    k = int(name[1])
                    dve.wait_ge(s["misc_full"], use + 1)
                    o = misc_f.rearrange("p (h w) -> p h w", w=VW)
                    nc.vector.reciprocal(sums_inv[:, k, :], o[:, :, DH]).then_inc(s["sums_ready"], 1)
                    dve.wait_ge(s["sums_ready"], CH * b + k + 1)
                    nc.vector.tensor_tensor(attn[:, k, :].rearrange("p (h d) -> p h d", h=H), o[:, :, 0:DH],
                                            sums_inv[:, k, :].unsqueeze(2).to_broadcast([P, H, DH]), ALU.mult).then_inc(s["attn_ready"], 1)
                elif name == "proj":
                    dve.wait_ge(s["misc_full"], use + 1)
                    row = x_all[:, bass.ds(b, 1), :, :].rearrange("p o k c -> p (o k c)")
                    nc.vector.tensor_tensor(row, misc_f, row, ALU.add).then_inc(s["x1_ready"], 1)
                elif name == "router":
                    logits = misc_f[:, 0:CH * E].rearrange("p (k e) -> p k e", e=E)
                    dve.wait_ge(s["misc_full"], use + 1)
                    nc.vector.tensor_reduce(r_max[:], logits, AX.X, ALU.max).then_inc(s["r_max_ready"], 1)
                    dve.wait_ge(s["r_max_ready"], b + 1)
                    nc.vector.tensor_tensor(r_logit[:], logits, r_max[:].unsqueeze(2).to_broadcast([P, CH, E]),
                                            ALU.subtract).then_inc(s["r_logit_ready"], 1)

            def ln2_stats(b, k):
                if k == 0:
                    dve.wait_ge(s["x1_ready"], b + 1)
                    dve.sem_inc(s["waited"])
                if k < CH - 1:
                    bn_stats(b, bn2, k)
                elif k < CH:
                    bn_stats(b, bn2, k).then_inc(s["ln2_bn"], 1)
                else:
                    bn_aggregate(b, bn2, mv2, "ln2_bn").then_inc(s["ln2_mv"], 1)

            def softmax_sum(b):
                dve.wait_ge(s["r_exp_ready"], b + 1)
                nc.vector.tensor_reduce(r_sum[:], r_exp[:], AX.X, ALU.add).then_inc(s["r_sum_ready"], 1)
                dve.wait_ge(s["r_sum_ready"], b + 1)
                nc.vector.reciprocal(r_inv[:], r_sum[:]).then_inc(s["r_inv_ready"], 1)

            def sort(b):
                dve.wait_ge(s["r_score_ready"], b + 1)
                dve.sem_inc(s["waited"])
                for k in range(CH):
                    last = nc.vector.max(r_sorted[:, k, :], r_score[:, k, 0:E])
                last.then_inc(s["r_sorted_ready"], 1)

            def pick(b):
                dve.wait_ge(s["r_top_ready"], b + 1)
                dve.sem_inc(s["waited"])
                for k in range(CH):
                    last = nc.vector.match_replace(r_without[:, k, :], r_top[:, k, :], r_score[:, k, :], 0.0)
                last.then_inc(s["r_without_ready"], 1)

            def denominator(b):
                dve.wait_ge(s["r_den_ready"], 2 * (b + 1))
                nc.vector.reciprocal(r_den_inv[:], r_den_eps[:]).then_inc(s["r_den_inv_ready"], 1)

            dve.wait_ge(s["x0_loaded"], 16)
            ln1_stats(0)
            dve.wait_ge(s["mod_full"], 1)
            nc.vector.tensor_copy(cT[:], s_col[0][:, 0:B]).then_inc(s["cT_ready"], 1)
            dve.wait_ge(s["wqkv_loaded"], 16)
            for i in range(2):
                last = nc.vector.tensor_copy(wqk_sb[:, i, :].rearrange("c (a d r) -> c a d r", a=2, d=DH),
                                             wqkv_sb[:, C * i:C * (i + 1)].rearrange("c (r a d) -> c a d r", a=2, d=DH))
            last.then_inc(s["wqk_ready"], 1)
            dve.wait_ge(s["mod_full"], 2)
            nc.vector.tensor_copy(mod[:].rearrange("p j b -> p (j b)"), s_col[1][:, 0:NJ * B]).then_inc(s["mod_step"], 1)
            dve.wait_ge(s["mod_step"], 1)
            nc.vector.tensor_scalar(mod[:, CA, :], mod[:, CA, :], 1.0, None, ALU.add)
            nc.vector.tensor_scalar(mod[:, CB, :], mod[:, CB, :], 1.0, None, ALU.add).then_inc(s["mod_ready"], 1)
            g, twice, size = mod[:, GA::GB - GA, :], mod_tmp[:, 0], mod_tmp[:, 1]
            nc.vector.tensor_scalar(twice, g, 0.0, 2.0, ALU.is_ge, ALU.mult).then_inc(s["mod_step"], 1)
            dve.wait_ge(s["mod_step"], 2)
            nc.vector.scalar_tensor_tensor(out=size, in0=twice, scalar=-1.0, in1=g, op0=ALU.add, op1=ALU.mult).then_inc(s["mod_step"], 1)
            dve.wait_ge(s["mod_step"], 3)
            nc.vector.tensor_scalar(size, size, GATE_MIN, None, ALU.max).then_inc(s["mod_step"], 1)
            dve.wait_ge(s["mod_step"], 4)
            nc.vector.scalar_tensor_tensor(out=g, in0=twice, scalar=-1.0, in1=size, op0=ALU.add, op1=ALU.mult).then_inc(s["mod_ready"], 1)

            dve.wait_ge(s["x_loaded"], 16)
            for name in PROJECT:
                evacuate(misc_use(0, None, None, name), 0, 0, name)
                if name == "k":
                    for b in range(1, B):
                        ln1_stats(b)
            dve.wait_ge(s["mod_full"], 3)
            for i, ga_ps in enumerate(ga_banks):
                last = nc.vector.tensor_copy(ga_rows[:, CH * i:CH * (i + 1), :].rearrange("p b c -> p (b c)"), ga_ps[:])
            last.then_inc(s["mod_ready"], 1)
            for t in range(AHEAD):
                for j in range(G):
                    row_max(0, 0, t, j)

            REST = {(1, 2): "q", (2, 2): "k"}
            LN2_STATS = [(6, 1), (7, 0), (7, 1), (8, 0), (8, 1)]
            ROUTE = {(12, 1): softmax_sum, (13, 0): sort, (13, 1): pick, (14, 0): denominator}

            def body(b, par, first, last):
                for t in range(SLOTS):
                    for half in range(3):
                        for j in range(2 * half, 2 * half + 2) if half < 2 else ():
                            if t < SLOTS - AHEAD:
                                row_max(b, par, t + AHEAD, j)
                            elif not last:
                                row_max(b + 1, 1 - par, t + AHEAD - SLOTS, j)
                            if (t, j) in REST and not last:
                                evacuate(None, b + 1, 1 - par, REST[t, j])
                        at = (t, half)
                        if not first:
                            if at in LN2_STATS:
                                ln2_stats(b - 1, LN2_STATS.index(at))
                            if at in ROUTE:
                                ROUTE[at](b - 1)
                        name = TASKS.get(at)
                        if name in tasks(first, last) and name not in REST.values():
                            of = owner(b, name)
                            evacuate(misc_use(b, first, last, name), of, 1 - par if of is not b else par, name)

            dve.wait_ge(s["top_const"], 1)
            over_batches(dve, body)

            def finish(b):
                dve.wait_ge(s["y_back"], b + 1)
                if not (isinstance(b, int) and b == 0):
                    dve.wait_ge(s["result_stored"], 16 * b)
                nc.vector.tensor_tensor(result, misc_f, x_all[:, bass.ds(b, 1), :, :].rearrange("p o k c -> p (o k c)"),
                                        ALU.add).then_inc(s["result_ready"], 1)

            def block_body(b, par, first, last):
                for k in range(KT):
                    i = KT * b + k
                    at = (par + k) % 2
                    name = TAIL_AT.get((k, 0))
                    if first and name:
                        evacuate(tail_use(TAIL.index(name)), B - 1, 1, name)
                    if first and k == 5:
                        dve.wait_ge(s["ln2_ready"], B)
                        for c in range(CH):
                            normal = nc.vector.tensor_scalar(x1n[:, c, :], x_all[:, B - 1, c, :], rstd2[:, c:c + 1], shift2[:, c:c + 1],
                                                             ALU.mult, ALU.add)
                        normal.then_inc(s["x1n_ready"], 1)
                    if first and k == 0:
                        evacuate(tail_use(0), B - 1, 1, TAIL_AT[0, 1])
                    dve.wait_ge(s["gate_acted"], i + 1)
                    dve.wait_ge(s["up_ready"], i + 1)
                    nc.vector.tensor_tensor(gated[at], gate_act[at], u_ps[at], ALU.mult).then_inc(s["gated_ready"], 1)
                    name = TAIL_AT.get((k, 1))
                    if first and k > 0 and name:
                        evacuate(tail_use(TAIL.index(name)), B - 1, 1, name)
                    if first and k == 8:
                        sort(B - 1)
                    dve.wait_ge(s["gated_ready"], i + 1)
                    dve.wait_ge(s[f"spread{k}_loaded"], 16 * len(EXPERT_ROWS[k]) * (b + 1))
                    if not (first and k < 2):
                        dve.wait_ge(s["hid_split"], i - 1)
                    nc.vector.tensor_tensor(weighed[at], gated[at], spread[k], ALU.mult).then_inc(s["weighed_ready"], 1)
                    if k == BACK + 1 and not first:
                        finish(b - 1)
                    if first:
                        if k == 3:
                            for step in range(CH + 1):
                                ln2_stats(B - 1, step)
                        elif k == 7:
                            softmax_sum(B - 1)
                        elif k == 8:
                            denominator(B - 1)
                            pick(B - 1)

            over_batches(dve, block_body)
            dve.wait_ge(s["hid_high"], KT * B)
            dve.wait_ge(s["hid_split"], KT * B - 1)
            nc.vector.tensor_tensor(hid_lo[(KT - 1) % HIDDEN][:], weighed[(B - 1 + KT - 1) % 2], hid_hi[(KT - 1) % HIDDEN][:],
                                    ALU.subtract).then_inc(s["hid_split"], 1)
            finish(B - 1)

        @block.tensor
        def _(pe):
            def free(b, name):
                if name == "xT":
                    pe.wait_ge(s["hT_ready"], b + 1)
                elif name == "q":
                    pe.wait_ge(s["q_rest_ready"], b + 1)
                elif name == "k":
                    pe.wait_ge(s["k_rest_ready"], b + 1)
                elif name == "v":
                    pe.wait_ge(s["v_ready"], b + 1)
                elif name.startswith("max"):
                    pe.wait_ge(s["maxT_ready"], group(b, int(name[3:])) + 1)
                elif name in ("o0", "o1", "o2", "o3"):
                    pe.wait_ge(s["attn_ready"], CH * b + int(name[1]) + 1)
                elif name == "attnT":
                    pe.wait_ge(s["attnT_ready"], b + 1)
                elif name == "proj":
                    pe.wait_ge(s["x1_ready"], b + 1)
                elif name == "x1T":
                    pe.wait_ge(s["h2T_ready"], b + 1)
                elif name == "router":
                    pe.wait_ge(s["r_logit_ready"], b + 1)
                elif name == "combT":
                    pe.wait_ge(s["combT_ready"], b + 2)

            def task(b, par, name):
                if name == "xT":
                    pe.wait_ge(s["xn_ready"], b + 1)
                    for k in range(CH):
                        last = nc.tensor.transpose(misc_f[:, P * k:P * (k + 1)], xn[:, k, :], ident[:])
                elif name == "q":
                    last = nc.tensor.matmul(misc_f, wqk_sb[:, 0, :], hT[:], start=True, stop=True)
                elif name == "k":
                    last = nc.tensor.matmul(k_bank(b), wqk_sb[:, 1, :], hT[:], start=True, stop=True)
                elif name == "v":
                    for k in range(CH):
                        last = nc.tensor.matmul(misc_f[:, C * k:C * (k + 1)], hT[:, P * k:P * (k + 1)], wqkv_sb[:, 2 * C:3 * C],
                                                start=True, stop=True)
                elif name.startswith("max"):
                    pe.wait_ge(s["max_split"], 4 * (group(b, int(name[3:])) + 1))
                    pe.sem_inc(s["waited"])
                    last = nc.tensor.transpose(misc_16[0:G * 3 * CH, 0:P], negmax_parts[:].rearrange("p g s k -> p (g s k)"), ident16[:])
                elif name in ("o0", "o1", "o2", "o3"):
                    k = int(name[1])
                    if k == 0:
                        pe.wait_ge(s["o_saved"], NG * (b + 1))
                    for n in range(NG):
                        last = nc.tensor.transpose(misc_f[:, P * n:P * (n + 1)], oT[par][:, n, P * k:P * (k + 1)], ident[:])
                elif name == "attnT":
                    for k in range(CH):
                        last = nc.tensor.transpose(misc_f[:, P * k:P * (k + 1)], attn[:, k, :], ident[:])
                elif name == "proj":
                    pe.wait_ge(s["attnT_ready"], b + 1)
                    pe.wait_ge(s["wo_ga_ready"], b + 1)
                    for k in range(CH):
                        last = nc.tensor.matmul(misc_f[:, C * k:C * (k + 1)], attnT[:, P * k:P * (k + 1)], wo_ga[:], start=True, stop=True)
                elif name == "x1T":
                    pe.wait_ge(s["x1n_ready"], b + 1)
                    for k in range(CH):
                        last = nc.tensor.transpose(misc_f[:, P * k:P * (k + 1)], x1n[:, k, :], ident[:])
                elif name == "router":
                    pe.wait_ge(s["wr_loaded"], 16)
                    for k in range(CH):
                        last = nc.tensor.matmul(misc_f[:, E * k:E * (k + 1)], h2T[:, P * k:P * (k + 1)], wr_sb[:], start=True, stop=True)
                elif name == "combT":
                    pe.wait_ge(s["comb_step"], 2 * (b + 1))
                    for k in range(CH):
                        last = nc.tensor.transpose(misc_f[0:E, P * k:P * (k + 1)], comb[:, k, :], ident[:])
                last.then_inc(s["misc_full"], 1)

            def row_scores(b, par, t, j):
                n, qc = t // CH, t % CH
                head = G * n + j
                u = G * t + j
                at = 64 * (head % 2)
                if t == 0 and j == 0:
                    pe.wait_ge(s["stacked_first"], 16 * LOADS * (b + 1))
                if t == CH and j == 0:
                    pe.wait_ge(s["stacked"], 16 * LOADS * (b + 1))
                if not (isinstance(b, int) and b == 0 and u < SCORES):
                    pe.wait_ge(s["row_max"], UNITS * b + u + 1 - score_distance("row", u))
                nc.tensor.matmul(s_row[score_bank("row", u)][:], q_stack[par][at:at + KS, head // 2, P * qc:P * (qc + 1)],
                                 k_stack[par][at:at + KS, head // 2, :], start=True, stop=True).then_inc(s["row_ready"], 1)

            def col_scores(b, par, t, j):
                n, kc = t // CH, t % CH
                head = G * n + j
                u = G * t + j
                at = 64 * (head % 2)
                if kc == 0 and j == 0:
                    pe.wait_ge(s["max_loaded"], 32 * (group(b, n) + 1))
                if not (isinstance(b, int) and b == 0 and u < SCORES):
                    pe.wait_ge(s["exp_done"], UNITS * b + u + 1 - score_distance("col", u))
                nc.tensor.matmul(s_col[score_bank("col", u)][:], k_stack[par][at:at + KS, head // 2, P * kc:P * (kc + 1)],
                                 q_stack[par][at:at + KS, head // 2, :], start=True, stop=True).then_inc(s["col_ready"], 1)

            def weigh(b, par, t):
                n, kc = t // CH, t % CH
                pe.wait_ge(s["exp_done"], UNITS * b + G * (t + 1))
                if kc == 0 and not (isinstance(b, int) and b == 0 and n == 0):
                    pe.wait_ge(s["o_saved"], group(b, n))
                for j in range(G):
                    last = nc.tensor.matmul(o_acc[VW * j:VW * (j + 1), :], v_aug[par][:, kc, G * n + j, :],
                                            probs[t % 2][:, j, :], start=(kc == 0), stop=(kc == CH - 1))
                last.then_inc(s["pv_done"], 1)

            pe.wait_ge(s["c_silu"], 1)
            pe.wait_ge(s["ident_ready"], 1)
            nc.tensor.transpose(s_col[0][:, 0:B], c_act[:], ident[0:B, 0:B]).then_inc(s["mod_full"], 1)
            pe.wait_ge(s["cT_ready"], 1)
            pe.wait_ge(s["wmod_loaded"], 16)
            for j in range(NJ):
                last = nc.tensor.matmul(s_col[1][:, B * j:B * (j + 1)], wmod_sb[:, C * j:C * (j + 1)], cT[:], start=True, stop=True)
            last.then_inc(s["mod_full"], 1)
            FIRST_ROWS = CH + 2
            for name in BEFORE:
                if name == "q":
                    pe.wait_ge(s["wqk_ready"], 1)
                if name == "v":
                    free(0, "q")
                elif name == "max0":
                    free(0, "k")
                    free(0, "v")
                elif name == "q":
                    free(0, "xT")
                if name == "max0":
                    pe.wait_ge(s["mod_ready"], 2)
                    for b in range(B):
                        last = nc.tensor.matmul(ga_banks[b // CH][:, C * (b % CH):C * (b % CH + 1)], mod[:, GA, b:b + 1].to_broadcast([C, P]), ident[:],
                                                start=True, stop=True)
                    last.then_inc(s["mod_full"], 1)
                    pe.wait_ge(s["ident16_ready"], 1)
                    for t in range(FIRST_ROWS):
                        for j in range(G):
                            row_scores(0, 0, t, j)
                task(0, 0, name)
            for t in range(FIRST_ROWS, AHEAD):
                for j in range(G):
                    row_scores(0, 0, t, j)
            pe.wait_ge(s["mod_ready"], 3)

            def body(b, par, first, last):
                mine = tasks(first, last)
                before = None

                def turn(at):
                    nonlocal before
                    name = TASKS.get(at)
                    if name not in mine:
                        return
                    if before is None:
                        free(b, "max0")
                        if not first:
                            pe.wait_ge(s["combT_ready"], b)
                    else:
                        free(owner(b, before), before)
                    of = owner(b, name)
                    task(of, par if of is b else 1 - par, name)
                    before = name

                for t in range(SLOTS):
                    def scores(j):
                        if t < SLOTS - AHEAD:
                            row_scores(b, par, t + AHEAD, j)
                        elif not last:
                            row_scores(b + 1, 1 - par, t + AHEAD - SLOTS, j)
                    for half in range(2):
                        for j in range(2 * half, 2 * half + 2):
                            scores(j)
                            col_scores(b, par, t, j)
                        turn((t, half))
                    if t > 0:
                        weigh(b, par, t - 1)
                    elif not first:
                        weigh(b - 1, 1 - par, SLOTS - 1)
                    turn((t, 2))

            over_batches(pe, body)

            pe.wait_ge(s["w_split"], 3)
            pe.wait_ge(s["row_max"], UNITS * B)

            def product(out_ps, w_hi, w_lo, k, hi, lo, start, stop):
                nc.tensor.matmul(out_ps, w_hi[:, k, :], hi[:], start=start, stop=False)
                nc.tensor.matmul(out_ps, w_hi[:, k, :], lo[:], start=False, stop=False)
                return nc.tensor.matmul(out_ps, w_lo[:, k, :], hi[:], start=False, stop=stop)

            def down(b, k):
                pe.wait_ge(s["hid_split"], KT * b + k + 1)
                if k == 0:
                    if isinstance(b, int) and b == 0:
                        pe.wait_ge(s["o_saved"], NG * B)
                    else:
                        pe.wait_ge(s["yT_ready"], b)
                product(y_ps, wd_hi, wd_lo, k, hid_hi[k % HIDDEN], hid_lo[k % HIDDEN],
                        start=(k == 0), stop=(k == KT - 1)).then_inc(s["down_done"], 1)

            def back(b):
                pe.wait_ge(s["yT_ready"], b + 1)
                if isinstance(b, int) and b == 0:
                    free(B - 1, "combT")
                else:
                    pe.wait_ge(s["result_ready"], b)
                for k in range(CH):
                    last = nc.tensor.transpose(misc_f[:, P * k:P * (k + 1)], yT[:, P * k:P * (k + 1)], ident[:])
                last.then_inc(s["y_back"], 1)

            def tail_task(name):
                if name is None:
                    return
                n = TAIL.index(name)
                if n:
                    free(B - 1, TAIL[n - 1])
                else:
                    free(B - 2, "combT")
                task(B - 1, 1, name)

            def block_body(b, par, first, last):
                for k in range(KT):
                    i = KT * b + k
                    at = (par + k) % 2
                    if k == 0:
                        pe.wait_ge(s["h_split"], b + 1)
                    if not (first and k < 2):
                        pe.wait_ge(s["gate_acted"], i - 1)
                    product(g_ps[at], wg_hi, wg_lo, k, h_hi[par], h_lo[par], True, True).then_inc(s["gate_ready"], 1)
                    if first and k == 0:
                        weigh(B - 1, 1, SLOTS - 1)
                    if first:
                        tail_task(TAIL_AT.get((k, 0)))
                    if not (first and k < 2):
                        pe.wait_ge(s["gated_ready"], i - 1)
                    product(u_ps[at], wu_hi, wu_lo, k, h_hi[par], h_lo[par], True, True).then_inc(s["up_ready"], 1)
                    if k >= LAG:
                        down(b, k - LAG)
                    elif not first:
                        down(b - 1, KT + k - LAG)
                    if k == BACK and not first:
                        back(b - 1)
                    if first:
                        tail_task(TAIL_AT.get((k, 1)))

            over_batches(pe, block_body)
            for k in range(KT - LAG, KT):
                down(B - 1, k)
            back(B - 1)


_INS = ['L0_attn_x', 'L0_attn_w_qkv', 'L0_attn_w_out', 'L0_ffn_w_router', 'L0_ffn_w_gate', 'L0_ffn_w_up', 'L0_ffn_w_down', 'L0_c', 'L0_wmod']


def kernel(**inputs):
    import concourse.bacc as bacc
    import numpy as np
    from concourse.bass_utils import run_bass_kernel_spmd

    nc = bacc.Bacc("TRN2", target_bir_lowering=False, num_devices=1)
    arrays, args = {}, []
    for name in _INS:
        a = np.ascontiguousarray(inputs[name])
        arrays[f"in_{name}"] = a
        args.append(nc.dram_tensor(f"in_{name}", a.shape, mybir.dt.from_np(a.dtype), kind="ExternalInput").ap())
    out = nc.dram_tensor("out", inputs["L0_attn_x"].shape, F32, kind="ExternalOutput").ap()
    adaln_block(nc, *args, out)
    return run_bass_kernel_spmd(nc, [arrays], core_ids=[0]).results[0]["out"]
```
